# Optimizing a Trainium2 kernel written in Bass

```python
import numpy as np
import jax
import jax.numpy as jnp

def _softmax(x, axis=-1):
    return jax.nn.softmax(x, axis=axis)

def _gelu(x):
    return jax.nn.gelu(x, approximate=True)

def _silu(x):
    return jax.nn.silu(x)

def _sigmoid(x):
    return jax.nn.sigmoid(x)

def _layernorm(x, axis=-1, eps=1e-05):
    m = jnp.mean(x, axis=axis, keepdims=True)
    v = jnp.var(x, axis=axis, keepdims=True)
    return (x - m) / jnp.sqrt(v + eps)

def _scatter_add(tgt, idx, src, axis=0):
    return tgt.at[idx].add(src)

def _segment_sum(src, seg, n):
    return jax.ops.segment_sum(src, seg, n)
kernel_name = 'mk_adj_resnorm_d4_adj_r2_c228e2'

def setup_inputs(seed: int=0):
    np.random.seed(seed)
    _w = jnp.asarray

    def _rec_inputs():
        import jax
        import jax.numpy as jnp
        _gk = jax.random.key(seed)
        x = -9.806e-05 + 1 * jax.random.normal(jax.random.fold_in(_gk, 1), (4096, 64), jnp.float32)
        _a = jax.random.bernoulli(jax.random.fold_in(_gk, 2), 0.000976562, (4096, 4096))
        _a = jnp.logical_or(_a, jnp.swapaxes(_a, -1, -2))
        _a = jnp.logical_or(_a, jnp.eye(4096, dtype=bool))
        adj = _a.astype(jnp.int32)
        return (x, adj)
    x, adj = _rec_inputs()

    def _L0_gnn_setup():
        import jax, jax.numpy as jnp
        import numpy as np
        ALPHA = 0.2
        NEG_BIG = -9000000000000000.0
        key = jax.random.key(seed)
        k1, k2, k3, k4, k5 = jax.random.split(key, 5)
        N, M, F_in, F_out = (4096, 4096, 64, 64)
        item_embs = jax.random.normal(k1, (N, F_in), dtype=jnp.float32)
        entity_embs = jax.random.normal(k2, (M, F_in), dtype=jnp.float32)
        adj = jax.random.randint(k3, (N, M), 0, 2, dtype=jnp.int32)
        W = jax.random.normal(k4, (F_in, F_out), dtype=jnp.float32)
        a = jax.random.normal(k5, (2 * F_out, 1), dtype=jnp.float32)
        return {'item_embs': item_embs, 'entity_embs': entity_embs, 'adj': adj, 'W': W, 'a': a}
    _L0_gnn_all = _L0_gnn_setup()
    _L0_gnn_in = {k: v for k, v in _L0_gnn_all.items() if k in ('entity_embs', 'W', 'a')}
    del _L0_gnn_all

    def _L1_gnn_setup():
        import jax, jax.numpy as jnp
        import numpy as np
        ALPHA = 0.2
        NEG_INF = -9000000000000000.0
        key = jax.random.key(seed)
        k1, k2, k3, k4 = jax.random.split(key, 4)
        N, F_IN, F_OUT = (512, 64, 64)
        h = jax.random.normal(k1, (N, F_IN), dtype=jnp.float32)
        adj = jax.random.randint(k2, (N, N), 0, 2, dtype=jnp.int32)
        lim_W = 1.414 * np.sqrt(6.0 / (F_IN + F_OUT))
        W = jax.random.uniform(k3, (F_IN, F_OUT), minval=-lim_W, maxval=lim_W, dtype=jnp.float32)
        lim_a = 1.414 * np.sqrt(6.0 / (2 * F_OUT + 1))
        a = jax.random.uniform(k4, (2 * F_OUT, 1), minval=-lim_a, maxval=lim_a, dtype=jnp.float32)
        return {'h': h, 'adj': adj, 'W': W, 'a': a}
    _L1_gnn_all = _L1_gnn_setup()
    _L1_gnn_in = {k: v for k, v in _L1_gnn_all.items() if k in ('W', 'a')}
    del _L1_gnn_all

    def _L2_gnn_setup():
        import jax, jax.numpy as jnp
        import numpy as np
        N = 4096
        D = 64
        NEG_INF = -9000000000000000.0
        LEAKY_SLOPE = 0.01
        key = jax.random.key(seed)
        k1, k2, k3 = jax.random.split(key, 3)
        h = jax.random.normal(k1, (N, D), dtype=jnp.float32)
        adj = jax.random.randint(k2, (N, N), 0, 2, dtype=jnp.int32)
        bound = float(np.sqrt(6.0 / (2 * D + 1)))
        a = jax.random.uniform(k3, (2 * D, 1), dtype=jnp.float32, minval=-bound, maxval=bound)
        return {'h': h, 'adj': adj, 'a': a}
    _L2_gnn_all = _L2_gnn_setup()
    _L2_gnn_in = {k: v for k, v in _L2_gnn_all.items() if k in ('a',)}
    del _L2_gnn_all

    def _L3_gnn_setup():
        import jax, jax.numpy as jnp
        import numpy as np
        ALPHA = 0.2
        MASK_VAL = -9000000000000000.0
        key = jax.random.key(seed)
        k1, k2, k3 = jax.random.split(key, 3)
        N, D = (4096, 64)
        h = jax.random.normal(k1, (N, D), dtype=jnp.float32)
        adj = jax.random.randint(k2, (N, N), 0, 2, dtype=jnp.int32)
        a = jax.random.normal(k3, (2 * D, 1), dtype=jnp.float32) * (1.414 / np.sqrt(D))
        return {'h': h, 'adj': adj, 'a': a}
    _L3_gnn_all = _L3_gnn_setup()
    _L3_gnn_in = {k: v for k, v in _L3_gnn_all.items() if k in ('a',)}
    del _L3_gnn_all
    return {'x': x, 'adj': adj, 'L0_gnn_entity_embs': _L0_gnn_in['entity_embs'], 'L0_gnn_W': _L0_gnn_in['W'], 'L0_gnn_a': _L0_gnn_in['a'], 'L1_gnn_W': _L1_gnn_in['W'], 'L1_gnn_a': _L1_gnn_in['a'], 'L2_gnn_a': _L2_gnn_in['a'], 'L3_gnn_a': _L3_gnn_in['a']}

def reference(x, adj, L0_gnn_entity_embs, L0_gnn_W, L0_gnn_a, L1_gnn_W, L1_gnn_a, L2_gnn_a, L3_gnn_a):
    import jax
    import jax.numpy as jnp

    def _L0_gnn_ref(item_embs, entity_embs, adj, W, a):
        import jax, jax.numpy as jnp
        import numpy as np
        ALPHA = 0.2
        NEG_BIG = -9000000000000000.0
        F_out = W.shape[1]
        Wh = item_embs @ W
        We = entity_embs @ W
        a1 = a[:F_out, 0]
        a2 = a[F_out:, 0]
        scores = (Wh @ a1)[:, None] + (We @ a2)[None, :]
        e = jnp.where(scores > 0, scores, ALPHA * scores)
        e = jnp.where(adj > 0, e, NEG_BIG)
        attention = jax.nn.softmax(e, axis=1)
        entity_emb_weighted = attention @ entity_embs
        h_prime = entity_emb_weighted + item_embs
        return jax.nn.elu(h_prime)

    def _L1_gnn_ref(h, adj, W, a):
        import jax, jax.numpy as jnp
        import numpy as np
        ALPHA = 0.2
        NEG_INF = -9000000000000000.0
        F_OUT = W.shape[1]
        Wh = h @ W
        a1, a2 = (a[:F_OUT, 0], a[F_OUT:, 0])
        e = (Wh @ a1)[:, None] + (Wh @ a2)[None, :]
        e = jax.nn.leaky_relu(e, negative_slope=ALPHA)
        scores = jnp.where(adj > 0, e, jnp.float32(NEG_INF))
        attention = jax.nn.softmax(scores, axis=1)
        h_prime = attention @ Wh
        return jax.nn.elu(h_prime)

    def _L2_gnn_ref(h, adj, a):
        import jax, jax.numpy as jnp
        import numpy as np
        N = 4096
        D = 64
        NEG_INF = -9000000000000000.0
        LEAKY_SLOPE = 0.01
        a1 = a[:D, 0]
        a2 = a[D:, 0]
        src = h @ a1
        dst = h @ a2
        e = src[:, None] + dst[None, :]
        e = jnp.where(e > 0, e, LEAKY_SLOPE * e)
        e = jnp.where(adj > 0, e, NEG_INF)
        attention = jax.nn.softmax(e, axis=1)
        h_prime = attention @ h
        return h_prime

    def _L3_gnn_ref(h, adj, a):
        import jax, jax.numpy as jnp
        import numpy as np
        ALPHA = 0.2
        MASK_VAL = -9000000000000000.0
        D = h.shape[1]
        wh1 = h @ a[:D, :]
        wh2 = h @ a[D:, :]
        e = wh1 + wh2.T
        e = jnp.where(e > 0, e, ALPHA * e)
        scores = jnp.where(adj > 0, e, MASK_VAL)
        attention = jax.nn.softmax(scores, axis=1)
        h_prime = attention @ h
        return jax.nn.relu(h_prime)
    x = _layernorm(x + _L0_gnn_ref(x, L0_gnn_entity_embs, adj, L0_gnn_W, L0_gnn_a), axis=-1)
    x = _layernorm(x + _L1_gnn_ref(x, adj, L1_gnn_W, L1_gnn_a), axis=-1)
    x = _layernorm(x + _L2_gnn_ref(x, adj, L2_gnn_a), axis=-1)
    x = _layernorm(x + _L3_gnn_ref(x, adj, L3_gnn_a), axis=-1)
    return x

_drawn_inputs = setup_inputs


def setup_inputs(seed=0):
    import zlib

    import numpy as np

    out = dict(_drawn_inputs(seed))
    spreads = {}
    factors = {}
    for name, (base, spread) in spreads.items():
        noise = np.random.default_rng([zlib.crc32(name.encode()), seed]).standard_normal(out[name].shape)
        drawn = base * np.exp(spread * noise) if base else spread * noise
        out[name] = jnp.asarray(drawn.astype(out[name].dtype))
    for name, factor in factors.items():
        out[name] = (out[name] * factor).astype(out[name].dtype)
    return out
```

```python
from contextlib import ExitStack

import concourse.bass as bass
from concourse import mybir

ALU = mybir.AluOpType
ACT = mybir.ActivationFunctionType
AX = mybir.AxisListType
F32 = mybir.dt.float32
BF16 = mybir.dt.bfloat16
U8 = mybir.dt.uint8
I32 = mybir.dt.int32
RMAX = bass.bass_isa.ReduceOp.max

P = 128
SLOPE = (0.2, 0.2, 0.01, 0.2)
ELU, NONE, RELU = "elu", "none", "relu"
OUTPUT = (ELU, ELU, NONE, RELU)
EPS = 1e-5
TINY = 1e-38
MAGIC = float(0x5F3759DF)


def build(nc, x, adj, ent, W0, a0, W1, a1, a2, a3, out):
    N, F = x.shape
    NB = N // P
    SB = 4
    NS = NB // SB
    CW = SB * P
    F1 = F + 1
    RING = 4
    CHUNK = 1024
    NCH = N // CHUNK
    LAYERS = 4

    ctx = ExitStack()
    with ctx:
        def sb(name, shape, dt):
            return ctx.enter_context(nc.sbuf_tensor(name, shape, dt))

        def ps(name):
            return ctx.enter_context(nc.psum_tensor(name, [P, 512], F32))

        def sem(name):
            return ctx.enter_context(nc.semaphore(name))

        h = [sb("h0", [P, NB, F1], F32), sb("h1", [P, NB, F1], F32)]
        agg = sb("agg", [P, NB, F1], F32)
        tmp = sb("tmp", [P, NB, F1], F32)
        identf = sb("identf", [P, P], F32)
        identb = sb("identb", [P, P], BF16)
        onesf = sb("onesf", [P, P], F32)
        picks = sb("picks", [65, P], BF16)
        wmat = sb("wmat", [F, 2, F], F32)
        acol = sb("acol", [F, LAYERS, 2], F32)
        arep = sb("arep", [F, P], F32)
        wt = sb("wt", [F, 2, F], F32)
        wrow = sb("wrow", [P, LAYERS, 2, F], F32)
        E = sb("E", [F1, 2, F1], F32)
        colsum = sb("colsum", [F1, P], F32)
        meanrow = sb("meanrow", [P, F1], F32)
        scol = sb("scol", [P, NB], F32)
        dcol = sb("dcol", [P, NB], F32)
        ycol = sb("ycol", [P, NB], F32)
        st = sb("st", [P, 8, NB], F32)
        ext = sb("ext", [P, 4], F32)
        exta = sb("exta", [P, 4], F32)
        drow = sb("drow", [P, N], F32)
        nat = sb("nat", [P, 2, SB, N], BF16)
        junk = sb("junk", [P, CHUNK], BF16)
        rmax = sb("rmax", [P, SB, NCH], F32)
        sm = sb("sm", [P, 8, SB], F32)
        diag = sb("diag", [P, 2, SB, P], F32)
        xrow = sb("xrow", [P, CW], F32)
        s2hi = sb("s2hi", [65, CW], BF16)
        s2r = sb("s2r", [65, CW], F32)
        s2mid = sb("s2mid", [65, CW], BF16)
        s2rows = sb("s2rows", [65, CW], BF16)
        U = sb("U", [P, RING, CW], F32)
        stg = sb("stg", [P, 2, NB, CW], U8)
        numT = sb("numT", [F1, CW], F32)

        Wp = [ps(f"Wp{i}") for i in range(RING)]
        acc = ps("acc")
        rowp = [ps("rowp0"), ps("rowp1")]
        natp = ps("natp")

        maskT = nc.dram_tensor("maskT", [NB, P, N], U8, kind="Internal").ap()

        loaded = sem("loaded")
        consts = sem("consts")
        setup_pe = sem("setup_pe")
        setup_dve = sem("setup_dve")
        setup_act = sem("setup_act")
        hready = sem("hready")
        stored = [sem("stored0"), sem("stored1")]
        out_ready = sem("out_ready")

        adj_v = adj.rearrange("(p b) j -> b p j", b=NB)
        nat_j = nat[:, :, :, :].rearrange("p h k (j b) -> p h k b j", b=NB)
        drow_b = drow[:, :].rearrange("p (j b) -> p b j", b=NB)
        x_v = x.rearrange("(p b) f -> p b f", b=NB)
        ent_v = ent.rearrange("(p b) f -> p b f", b=NB)
        out_v = out.rearrange("(p b) f -> p b f", b=NB)
        mask_v = maskT.rearrange("b p i -> p b i")

        L = []
        for l in range(LAYERS):
            L.append({n: sem(f"{n}_{l}") for n in (
                "ext_ready", "ext_all", "diag_d", "drow_mm", "drow_ok", "cs_mm", "cs_ok", "mr_mm", "mr_ok",
                "landed0", "landed1", "landed2", "landed3", "landed4", "landed5", "landed6", "landed7",
                "binned", "diag_ok", "rows_mm", "rows_ev", "res_ok", "rows_ok", "turned", "saved",
                "w_full", "u_full", "p_full", "acc_full", "numt_ok", "nat_mm", "agg_ok",
                "elu_in", "elu_out", "layer")})

        block = ctx.enter_context(nc.Block())

        def src(l):
            return 1 if l == 0 else (l + 1) % 2

        def res(l):
            return 0 if l == 0 else (l + 1) % 2

        def dst(l):
            return 0 if l == 0 else l % 2

        @block.sync
        def _(sp):
            sp.dma_start(h[0][:, :, 0:F], x_v).then_inc(loaded, 16)
            sp.dma_start(h[1][:, :, 0:F], ent_v).then_inc(loaded, 16)
            sp.dma_start(wmat[:, 0, :], W0).then_inc(loaded, 16)
            sp.dma_start(wmat[:, 1, :], W1).then_inc(loaded, 16)
            for l, a in enumerate((a0, a1, a2, a3)):
                for t in range(2):
                    sp.dma_start(acol[:, l, t:t + 1], a[F * t:F * t + F, :]).then_inc(loaded, 16)
            for half in range(2):
                sp.sem_inc(stored[half], 16)
            for l in range(LAYERS):
                S = L[l]
                with sp.Fori(0, N - 2 * CW + 1, 2 * CW) as i0:
                    for half in range(2):
                        sp.wait_ge(S["saved"], i0 + (half + 1) * CW)
                        sp.dma_start(mask_v[:, :, bass.ds(i0 + half * CW, CW)], stg[:, half]).then_inc(
                            stored[half], 16)
            sp.wait_ge(L[LAYERS - 1]["layer"], 1)
            sp.dma_start(out_v, h[dst(LAYERS - 1)][:, :, 0:F]).then_inc(out_ready, 16)
            sp.wait_ge(out_ready, 16)
            for half in range(2):
                sp.wait_ge(stored[half], 16 + 16 * NS // 2 * LAYERS)

        @block.gpsimd
        def _(pool):
            nc.gpsimd.memset(identf[:], 0.0).then_inc(consts, 1)
            pool.wait_ge(consts, 1)
            nc.gpsimd.affine_select(out=identf[:], in_=identf[:], compare_op=ALU.not_equal, fill=1.0, base=0,
                                    pattern=[[-1, P]], channel_multiplier=1).then_inc(consts, 1)
            for l in range(LAYERS):
                S = L[l]

                def load(s, half):
                    for k in range(SB):
                        pool.dma_start(nat[:, half, k, :], adj_v[s * SB + k]).then_inc(
                            S[f"landed{half * SB + k}"], 16)

                if l:
                    pool.wait_ge(L[l - 1]["layer"], 1)
                load(0, 0)
                pool.wait_ge(S["ext_ready"], 1)
                nc.gpsimd.partition_all_reduce(exta[:, 0:2], ext[:, 0:2], P, RMAX).then_inc(S["ext_all"], 1)
                with pool.Fori(0, NS // 2) as J:
                    pool.wait_ge(S["turned"], J * 2 * NB + NB)
                    load(J * 2 + 1, 1)
                    pool.wait_ge(S["turned"], J * 2 * NB + 2 * NB)
                    load((J * 2 + 2) % NS, 0)

        @block.tensor
        def _(pe):
            pe.wait_ge(setup_dve, 1)
            for m in range(2):
                nc.tensor.matmul(rowp[0][0:F, F * m:F * m + F], wmat[:, m, :], identf[0:F, 0:F],
                                 start=True, stop=True).then_inc(setup_pe, 1)
            for l in range(LAYERS):
                for t in range(2):
                    n = 2 * l + t
                    pe.wait_ge(setup_dve, 2 + n)
                    rhs = wt[:, l, :] if l < 2 else identf[0:F, 0:F]
                    nc.tensor.matmul(rowp[1][:, 0:F], arep[:, :], rhs, start=True, stop=True).then_inc(setup_pe, 1)
            for l in range(LAYERS):
                S = L[l]
                V = h[src(l)]
                e = E[:, 1 if l == 1 else 0, :]
                pe.wait_ge(hready, l + 1)
                pe.sem_inc(S["turned"], NB)
                for b in range(NB):
                    mm = nc.tensor.matmul(natp[0:F1, 0:P], V[:, b, :], onesf[:, :], start=(b == 0), stop=(b == NB - 1))
                mm.then_inc(S["cs_mm"], 1)
                pe.wait_ge(S["cs_ok"], 1)
                nc.tensor.matmul(natp[:, 0:F1], colsum[:, :], e, start=True, stop=True).then_inc(S["mr_mm"], 1)
                for c in range(N // CW):
                    pe.wait_ge(S["diag_d"], c + 1)
                    if c >= 2:
                        pe.wait_ge(S["drow_ok"], c - 1)
                    nc.tensor.matmul(rowp[c % 2][:, :], onesf[:, :], diag[:, c % 2], start=True, stop=True).then_inc(
                        S["drow_mm"], 1)
                with pe.Fori(0, NS // 2) as J:
                    for half in range(2):
                        s = J * 2 + half
                        pe.wait_ge(S["diag_ok"], s + 1)
                        for q in range(2):
                            mm = nc.tensor.matmul(rowp[q][:, :], onesf[:, :], diag[:, q], start=True, stop=True)
                        mm.then_inc(S["rows_mm"], 1)
                        pe.wait_ge(S["binned"], s * SB + SB)
                        for t in range(NB + 3):
                            if t < NB:
                                for k in range(SB):
                                    mm = nc.tensor.matmul(Wp[t % RING][:, P * k:P * k + P], nat_j[:, half, k, t, :],
                                                          identb[:, :], start=(k == 0), stop=True,
                                                          skip_group_check=True)
                                mm.then_inc(S["turned"], 1)
                            if 0 <= t - 1 < NB:
                                if t == 1:
                                    pe.wait_ge(S["rows_ok"], s + 1)
                                pe.wait_ge(S["saved"], (s * NB + t) * (CW // NB))
                                nc.tensor.matmul(Wp[(t - 1) % RING][:, :], picks[:, :], s2rows[:, :], start=False,
                                                 stop=True, skip_group_check=True).then_inc(S["w_full"], 1)
                            if 0 <= t - 3 < NB:
                                b = t - 3
                                pe.wait_ge(S["p_full"], s * NB + b + 1)
                                mm = nc.tensor.matmul(acc[0:F1, :], V[:, b, :], U[:, b % RING, :], start=(b == 0),
                                                      stop=(b == NB - 1))
                        mm.then_inc(S["acc_full"], 1)
                        pe.wait_ge(S["numt_ok"], s + 1)
                        for k in range(SB):
                            mm = nc.tensor.matmul(natp[:, F1 * k:F1 * k + F1], numT[:, P * k:P * k + P], e,
                                                  start=True, stop=True)
                        mm.then_inc(S["nat_mm"], 1)

        @block.scalar
        def _(act):
            for l in range(LAYERS):
                S = L[l]
                act.wait_ge(S["cs_mm"], 1)
                nc.scalar.activation(colsum[:, :], natp[0:F1, 0:P], ACT.Copy).then_inc(S["cs_ok"], 1)
                act.wait_ge(S["mr_mm"], 1)
                nc.scalar.activation(meanrow[:, :], natp[:, 0:F1], ACT.Copy).then_inc(S["mr_ok"], 1)
                for c in range(N // CW):
                    act.wait_ge(S["drow_mm"], c + 1)
                    nc.scalar.activation(drow_b[:, SB * c:SB * c + SB, :],
                                         rowp[c % 2][:, :].rearrange("p (b j) -> p b j", b=SB), ACT.Copy).then_inc(
                        S["drow_ok"], 1)
                with act.Fori(0, NS // 2) as J:
                    for half in range(2):
                        s = J * 2 + half
                        act.wait_ge(stored[half], 16 * NS // 2 * l + 16 * J + 16)
                        act.wait_ge(S["rows_mm"], s + 1)
                        nc.scalar.activation(s2hi[:, :], rowp[0][0:65, :], ACT.Copy).then_inc(S["rows_ev"], 1)
                        nc.scalar.activation(s2rows[0:1, :], rowp[0][0:1, :], ACT.Copy).then_inc(S["rows_ev"], 1)
                        nc.scalar.activation(xrow[:, :], rowp[1][:, :], ACT.Copy).then_inc(S["rows_ev"], 1)
                        for t in range(NB + 2):
                            if t < NB:
                                act.wait_ge(S["turned"], s * NB + t + 1 + NB)
                                nc.scalar.activation(stg[:, half, t, :], Wp[t % RING][:, :], ACT.Relu,
                                                     bias=1.0).then_inc(S["saved"], CW // NB)
                            if t >= 2:
                                b = t - 2
                                act.wait_ge(S["u_full"], s * NB + b + 1)
                                nc.scalar.activation(U[:, b % RING, :], U[:, b % RING, :], ACT.Exp,
                                                     bias=dcol[:, b:b + 1]).then_inc(S["p_full"], 1)
                        act.wait_ge(S["acc_full"], s + 1)
                        nc.scalar.activation(numT[:, :], acc[0:F1, :], ACT.Copy).then_inc(S["numt_ok"], 1)
                        act.wait_ge(S["nat_mm"], s + 1)
                        nc.scalar.activation(agg[:, bass.ts(s, SB), :],
                                             natp[:, 0:SB * F1].rearrange("p (k f) -> p k f", k=SB),
                                             ACT.Copy).then_inc(S["agg_ok"], 1)
                if OUTPUT[l] == ELU:
                    act.wait_ge(S["elu_in"], 1)
                    nc.scalar.activation(tmp[:, :, 0:F], tmp[:, :, 0:F], ACT.Exp).then_inc(S["elu_out"], 1)

        @block.vector
        def _(dve):
            v = nc.vector

            def then_drain(_):
                dve.drain()

            def rows_of(col, n):
                return col.unsqueeze(2).to_broadcast([P, n, F])

            def scores(l):
                for t, (node, col) in enumerate(((h[res(l)], scol), (h[src(l)], dcol))):
                    v.tensor_tensor(tmp[:, :, 0:F], node[:, :, 0:F],
                                    wrow[:, l, t, :].unsqueeze(1).to_broadcast([P, NB, F]), ALU.mult)
                    dve.drain()
                    v.tensor_reduce(col[:, :], tmp[:, :, 0:F], AX.X, ALU.add)
                    dve.drain()
                v.tensor_scalar(ycol[:, :], dcol[:, :], -(1.0 - SLOPE[l]), None, ALU.mult)
                v.tensor_reduce(ext[:, 0:1], dcol[:, :], AX.X, ALU.max)
                v.tensor_reduce(ext[:, 1:2], dcol[:, :], AX.X, ALU.min, negate=True)
                dve.drain().then_inc(L[l]["ext_ready"], 1)

            v.memset(onesf[:], 1.0)
            v.memset(picks[:], 0.0)
            v.memset(s2rows[:], 0.0)
            for b in range(2):
                v.memset(h[b][:, :, F:F1], 1.0)
            dve.drain()
            for r in (0, 32, 64):
                v.memset(picks[r:r + 1, :], 1.0)
            dve.wait_ge(consts, 2)
            v.tensor_copy(identb[:], identf[:])
            dve.wait_ge(loaded, 16 * 12)
            for m in range(2):
                v.tensor_copy(E[:, m, :], identf[0:F1, 0:F1])
            dve.drain()
            v.tensor_copy(E[0:F, 1, 0:F], wmat[:, 1, :])
            dve.drain().then_inc(setup_dve, 1)
            dve.wait_ge(setup_pe, 2)
            v.tensor_copy(wt[:, :, :], rowp[0][0:F, 0:2 * F].rearrange("p (m f) -> p m f", m=2))
            for l in range(LAYERS):
                for t in range(2):
                    n = 2 * l + t
                    v.tensor_scalar(arep[:, :], onesf[0:F, :], acol[:, l, t:t + 1], None, ALU.mult)
                    dve.drain().then_inc(setup_dve, 1)
                    dve.wait_ge(setup_pe, 3 + n)
                    v.tensor_copy(wrow[:, l, t, :], rowp[1][:, 0:F])
                    dve.drain()
            scores(0)
            dve.drain().then_inc(hready, 1)

            for l in range(LAYERS):
                S = L[l]
                slope = SLOPE[l]
                for c in range(NB // SB):
                    if c >= 2:
                        dve.wait_ge(S["drow_mm"], c - 1)
                    v.tensor_tensor(diag[:, c % 2], identf[:, :].unsqueeze(1).to_broadcast([P, SB, P]),
                                    dcol[:, SB * c:SB * c + SB].unsqueeze(2).to_broadcast([P, SB, P]),
                                    ALU.mult).then_inc(S["diag_d"], 1)
                dve.wait_ge(S["ext_all"], 1)
                v.tensor_tensor(ext[:, 2:3], exta[:, 0:1], exta[:, 1:2], ALU.add)
                dve.drain()
                v.tensor_scalar(ext[:, 3:4], ext[:, 2:3], -2.0, -256.0, ALU.mult, ALU.add)
                v.tensor_scalar(exta[:, 2:3], exta[:, 1:2], -1.0, None, ALU.mult)
                dve.drain()
                dve.wait_ge(S["drow_ok"], N // CW)
                dve.wait_ge(S["drow_mm"], N // CW)

                def binarise(half, k, turn):
                    dve.wait_ge(S[f"landed{half * SB + k}"], turn)
                    v.tensor_scalar(nat[:, half, k, :], nat[:, half, k, :], 0.0, ext[:, 3:4], ALU.is_le, ALU.mult)
                    dve.drain().then_inc(S["binned"], 1)

                def row_max(half, k, c):
                    dve.drain()
                    v.tensor_tensor_reduce(junk[:, :], nat[:, half, k, CHUNK * c:CHUNK * c + CHUNK],
                                           drow[:, CHUNK * c:CHUNK * c + CHUNK], 1.0, -3.0e38, ALU.add, ALU.max,
                                           rmax[:, k, c:c + 1])

                def row_terms(s):
                    dve.drain()
                    v.tensor_reduce(sm[:, 0, :], rmax[:, :, :], AX.X, ALU.max)
                    dve.drain()
                    v.tensor_scalar(sm[:, 1, :], sm[:, 0, :], exta[:, 2:3], None, ALU.max)
                    dve.drain()
                    sc = scol[:, bass.ts(s, SB)]
                    v.tensor_tensor(sm[:, 2, :], sm[:, 1, :], sc, ALU.add)
                    dve.drain()
                    v.scalar_tensor_tensor(out=sm[:, 3, :], in0=sm[:, 2, :], scalar=slope, in1=sm[:, 2, :],
                                           op0=ALU.mult, op1=ALU.max)
                    dve.drain()
                    v.scalar_tensor_tensor(out=sm[:, 4, :], in0=sc, scalar=slope, in1=sm[:, 3, :],
                                           op0=ALU.mult, op1=ALU.subtract)
                    v.tensor_scalar(sm[:, 5, :], sc, 1.0 - slope, None, ALU.mult)
                    dve.drain()
                    v.tensor_tensor(diag[:, :, :, :].rearrange("p q k j -> p (q k) j"),
                                    identf[:, :].unsqueeze(1).to_broadcast([P, 2 * SB, P]),
                                    sm[:, 4:6, :].rearrange("p q k -> p (q k)").unsqueeze(2).to_broadcast(
                                        [P, 2 * SB, P]), ALU.mult).then_inc(S["diag_ok"], 1)

                for k in range(SB):
                    binarise(0, k, 16)
                    for c in range(NCH):
                        row_max(0, k, c)
                row_terms(0)
                with dve.Fori(0, NS // 2) as J:
                    for half in range(2):
                        s = J * 2 + half
                        dve.wait_ge(S["rows_ev"], 3 * s + 3)
                        v.tensor_tensor(s2r[:, :], rowp[0][0:65, :], s2hi[:, :], ALU.subtract)
                        dve.drain()
                        v.tensor_copy(s2mid[:, :], s2r[:, :])
                        dve.drain()
                        v.tensor_copy(s2rows[32:33, :], s2mid[32:33, :])
                        v.tensor_tensor(s2rows[64:65, :], s2r[64:65, :], s2mid[64:65, :], ALU.subtract)
                        dve.drain().then_inc(S["rows_ok"], 1)
                        for t in range(NB):
                            dve.wait_ge(S["w_full"], s * NB + t + 1)
                            v.scalar_tensor_tensor(out=U[:, t % RING, :], in0=xrow[:, :], scalar=ycol[:, t:t + 1],
                                                   in1=Wp[t % RING][:, :], op0=ALU.max,
                                                   op1=ALU.add).then_inc(S["u_full"], 1)
                            if t % 8 == 0:
                                binarise(1 - half, t // 8, 16 * J + (16 if half == 0 else 32))
                            if t % 2 == 1:
                                row_max(1 - half, t // 8, t % 8 // 2)
                        row_terms((s + 1) % NS)
                dve.wait_ge(S["agg_ok"], NS)
                dve.wait_ge(S["mr_ok"], 1)
                den = agg[:, :, F:F1].rearrange("p b o -> p (b o)")
                v.tensor_scalar(st[:, 0, :], den, 0.0, None, ALU.is_le)
                dve.drain()
                v.tensor_tensor(tmp[:, :, :], st[:, 0, :].unsqueeze(2).to_broadcast([P, NB, F1]),
                                meanrow[:, :].unsqueeze(1).to_broadcast([P, NB, F1]), ALU.mult)
                dve.drain()
                v.tensor_tensor(agg[:, :, :], agg[:, :, :], tmp[:, :, :], ALU.add)
                dve.drain()
                v.reciprocal(st[:, 1, :], den)
                dve.drain()
                A = agg[:, :, 0:F]
                Z = tmp[:, :, 0:F]
                H = h[res(l)][:, :, 0:F]
                v.tensor_tensor(A, A, rows_of(st[:, 1, :], NB), ALU.mult)
                dve.drain()
                if l == 0:
                    v.tensor_tensor(A, A, H, ALU.add)
                    dve.drain()
                if OUTPUT[l] == ELU:
                    v.tensor_scalar(Z, A, 0.0, None, ALU.min)
                    dve.drain().then_inc(S["elu_in"], 1)
                    dve.wait_ge(S["elu_out"], 1)
                    v.scalar_tensor_tensor(out=A, in0=A, scalar=0.0, in1=Z, op0=ALU.max, op1=ALU.add)
                    dve.drain()
                    v.scalar_tensor_tensor(out=A, in0=A, scalar=-1.0, in1=H, op0=ALU.add, op1=ALU.add)
                elif OUTPUT[l] == RELU:
                    v.scalar_tensor_tensor(out=A, in0=A, scalar=0.0, in1=H, op0=ALU.max, op1=ALU.add)
                else:
                    v.tensor_tensor(A, A, H, ALU.add)
                dve.drain()
                v.tensor_reduce(st[:, 2, :], A, AX.X, ALU.add)
                dve.drain()
                v.tensor_scalar(st[:, 3, :], st[:, 2, :], 1.0 / F, None, ALU.mult)
                dve.drain()
                v.tensor_tensor(A, A, rows_of(st[:, 3, :], NB), ALU.subtract)
                dve.drain()
                v.tensor_tensor(Z, A, A, ALU.mult)
                dve.drain()
                v.tensor_reduce(st[:, 4, :], Z, AX.X, ALU.add)
                dve.drain()
                v.tensor_scalar(st[:, 5, :], st[:, 4, :], 1.0 / F, EPS, ALU.mult, ALU.add)
                dve.drain()
                v.tensor_scalar(st[:, 6, :].bitcast(I32), st[:, 5, :].bitcast(I32), 1, None,
                                ALU.logical_shift_right)
                dve.drain()
                v.tensor_scalar(st[:, 7, :].bitcast(I32), st[:, 6, :].bitcast(I32), -1.0, MAGIC, ALU.mult, ALU.add)
                dve.drain()
                for _ in range(4):
                    v.tensor_tensor(st[:, 6, :], st[:, 7, :], st[:, 7, :], ALU.mult)
                    dve.drain()
                    v.scalar_tensor_tensor(out=st[:, 6, :], in0=st[:, 6, :], scalar=-0.5, in1=st[:, 5, :],
                                           op0=ALU.mult, op1=ALU.mult)
                    dve.drain()
                    v.scalar_tensor_tensor(out=st[:, 7, :], in0=st[:, 6, :], scalar=1.5, in1=st[:, 7, :],
                                           op0=ALU.add, op1=ALU.mult)
                    dve.drain()
                v.tensor_tensor(h[dst(l)][:, :, 0:F], A, rows_of(st[:, 7, :], NB), ALU.mult)
                dve.drain().then_inc(S["layer"], 1)
                if l + 1 < LAYERS:
                    scores(l + 1)
                    dve.drain().then_inc(hready, 1)


_INS = ["x", "adj", "L0_gnn_entity_embs", "L0_gnn_W", "L0_gnn_a", "L1_gnn_W", "L1_gnn_a", "L2_gnn_a", "L3_gnn_a"]


def kernel(**inputs):
    import numpy as _np
    import concourse.bacc as _bacc
    from concourse import mybir as _mybir
    from concourse.bass_utils import run_bass_kernel_spmd as _run

    nc = _bacc.Bacc("TRN2", target_bir_lowering=False, num_devices=1)
    arrays, args = {}, []
    for name in _INS:
        a = _np.ascontiguousarray(inputs[name])
        arrays[f"in_{name}_dram"] = a
        args.append(nc.dram_tensor(f"in_{name}_dram", a.shape, _mybir.dt.from_np(a.dtype), kind="ExternalInput").ap())
    shape = inputs["x"].shape
    res = nc.dram_tensor("out_dram", shape, _mybir.dt.float32, kind="ExternalOutput").ap()
    build(nc, *args, res)
    r = _run(nc, [arrays], core_ids=[0])
    return r.results[0]["out_dram"]
```

```python
from contextlib import ExitStack

import concourse.bass as bass
from concourse import mybir

ALU = mybir.AluOpType
ACT = mybir.ActivationFunctionType
AX = mybir.AxisListType
F32 = mybir.dt.float32
BF16 = mybir.dt.bfloat16
U8 = mybir.dt.uint8
I32 = mybir.dt.int32
RMAX = bass.bass_isa.ReduceOp.max

P = 128
SLOPE = (0.2, 0.2, 0.01, 0.2)
ELU, NONE, RELU = "elu", "none", "relu"
OUTPUT = (ELU, ELU, NONE, RELU)
EPS = 1e-5
ROWS_AT = (2, 4, 14, 22)
FAST_RANGE = 60.0
TINY = 1e-38
MAGIC = float(0x5F3759DF)


def build(nc, x, adj, ent, W0, a0, W1, a1, a2, a3, out):
    N, F = x.shape
    NB = N // P
    SB = 4
    NS = NB // SB
    CW = SB * P
    F1 = F + 1
    RING = 4
    CHUNK = 1024
    NCH = N // CHUNK
    LAYERS = 4
    HALF = N // 2
    TR = 4
    MR = 8
    HB = NB // 2

    ctx = ExitStack()
    with ctx:
        def sb(name, shape, dt):
            return ctx.enter_context(nc.sbuf_tensor(name, shape, dt))

        def ps(name):
            return ctx.enter_context(nc.psum_tensor(name, [P, 512], F32))

        def sem(name):
            return ctx.enter_context(nc.semaphore(name))

        h = [sb("h0", [P, NB, F1], F32), sb("h1", [P, NB, F1], F32)]
        agg = sb("agg", [P, NB, F1], F32)
        tmp = sb("tmp", [P, NB, F1], F32)
        identf = sb("identf", [P, P], F32)
        identb = sb("identb", [P, P], BF16)
        onesf = sb("onesf", [P, P], F32)
        picks = sb("picks", [65, P], BF16)
        wmat = sb("wmat", [F, 2, F], F32)
        acol = sb("acol", [F, LAYERS, 2], F32)
        arep = sb("arep", [F, P], F32)
        wt = sb("wt", [F, 2, F], F32)
        wrow = sb("wrow", [P, LAYERS, 2, F], F32)
        E = sb("E", [F1, 2, F1], F32)
        colsum = sb("colsum", [F1, P], F32)
        meanrow = sb("meanrow", [P, F1], F32)
        scol = sb("scol", [P, NB], F32)
        dcol = sb("dcol", [P, NB], F32)
        ycol = sb("ycol", [P, NB], F32)
        st = sb("st", [P, 8, NB], F32)
        ext = sb("ext", [P, 4], F32)
        exta = sb("exta", [P, 4], F32)
        drow = sb("drow", [P, N], F32)
        nat = sb("nat", [P, 2, SB, N], BF16)
        junk = sb("junk", [P, CHUNK], BF16)
        rmax = sb("rmax", [P, SB, NCH], F32)
        sm = sb("sm", [P, 8, SB], F32)
        diag = sb("diag", [P, 2, SB, P], F32)
        xrow = sb("xrow", [P, CW], F32)
        s2hi = sb("s2hi", [65, CW], BF16)
        s2r = sb("s2r", [65, CW], F32)
        s2mid = sb("s2mid", [65, CW], BF16)
        s2rows = sb("s2rows", [65, CW], BF16)
        U = sb("U", [P, RING, CW], F32)
        stg = sb("stg", [P, 2, NB, CW], U8)
        numT = sb("numT", [F1, CW], F32)
        numF = sb("numF", [P, HALF], F32)
        choice = sb("choice", [P, 1], I32)
        qcol = sb("qcol", [P, NB], F32)
        wcol = sb("wcol", [P, NB], F32)
        rcol = sb("rcol", [P, NB], F32)
        VW = sb("VW", [P, NB, F], F32)
        MT = sb("MT", [F, 2 * F], F32)
        EF = sb("EF", [P, 2, F1], F32)
        T = nat[:, 0].rearrange("p k j -> p (k j)").bitcast(F32).rearrange("p (t i) -> p t i", t=TR)
        mring = stg[:, 0].rearrange("p b i -> p (b i)").rearrange("p (t i) -> p t i", i=HALF)

        Wp = [ps(f"Wp{i}") for i in range(RING)]
        acc = ps("acc")
        rowp = [ps("rowp0"), ps("rowp1")]
        natp = ps("natp")

        maskT = nc.dram_tensor("maskT", [P, NB * N], U8, kind="Internal").ap()

        loaded = sem("loaded")
        consts = sem("consts")
        setup_pe = sem("setup_pe")
        setup_dve = sem("setup_dve")
        setup_act = sem("setup_act")
        hready = sem("hready")
        out_ready = sem("out_ready")

        adj_v = adj.rearrange("(p b) j -> b p j", b=NB)
        nat_j = nat[:, :, :, :].rearrange("p h k (j b) -> p h k b j", b=NB)
        drow_b = drow[:, :].rearrange("p (j b) -> p b j", b=NB)
        x_v = x.rearrange("(p b) f -> p b f", b=NB)
        ent_v = ent.rearrange("(p b) f -> p b f", b=NB)
        out_v = out.rearrange("(p b) f -> p b f", b=NB)
        mask_v = maskT.rearrange("p (b i) -> p b i", b=NB)

        first_path_sem = sem("paths")
        path = {n: sem(n) for n in (
            "diag_d", "drow_mm", "drow_ok", "cs_mm", "cs_ok", "mr_mm", "mr_ok",
            "binned", "diag_ok", "rows_mm", "rows_ev", "rows_ok", "turned", "saved", "stored0", "stored1",
            "w_full", "u_full", "p_full", "acc_full", "numt_ok", "nat_mm", "agg_ok",
            "f_in", "f_exp", "f_vw", "f_diag", "f_rmm", "f_row", "f_t", "f_pv", "f_num",
            "f_nat") + tuple(f"f_mask{i}" for i in range(MR))}
        L = [path | {n: sem(f"{n}_{l}") for n in (
            "ext_ready", "ext_all", "choice", "elu_in", "elu_out", "layer", "left", "go") + tuple(
                f"landed{i}" for i in range(2 * SB))} for l in range(LAYERS)]

        block = ctx.enter_context(nc.Block())

        def src(l):
            return 1 if l == 0 else (l + 1) % 2

        def res(l):
            return 0 if l == 0 else (l + 1) % 2

        def dst(l):
            return 0 if l == 0 else l % 2

        def branch(eng, l, general, fast):
            if l == 0:
                general(l)
                return
            eng.wait_ge(L[l]["choice"], 1)
            eng.wait_ge(L[l - 1]["go"], 1)
            narrow = eng.value_load(choice[0:1, 0:1], min_val=0, max_val=1)
            with eng.If(narrow):
                fast(l)
            with eng.Else():
                general(l)

        @block.sync
        def _(sp):
            sp.dma_start(h[0][:, :, 0:F], x_v).then_inc(loaded, 16)
            sp.dma_start(h[1][:, :, 0:F], ent_v).then_inc(loaded, 16)
            sp.dma_start(wmat[:, 0, :], W0).then_inc(loaded, 16)
            sp.dma_start(wmat[:, 1, :], W1).then_inc(loaded, 16)
            for l, a in enumerate((a0, a1, a2, a3)):
                for t in range(2):
                    sp.dma_start(acol[:, l, t:t + 1], a[F * t:F * t + F, :]).then_inc(loaded, 16)

            def general(l):
                S = L[l]
                for half in range(2):
                    sp.sem_inc(S[f"stored{half}"], 16)
                with sp.Fori(0, N - 2 * CW + 1, 2 * CW) as i0:
                    for half in range(2):
                        sp.wait_ge(S["saved"], i0 + (half + 1) * CW)
                        sp.dma_start(mask_v[:, :, bass.ds(i0 + half * CW, CW)], stg[:, half]).then_inc(
                            S[f"stored{half}"], 16)
                for half in range(2):
                    sp.wait_ge(S[f"stored{half}"], 16 + 16 * NS // 2)

            def fast(l):
                S = L[l]
                for half in range(2):
                    with sp.Fori(0, NB * N - MR * N + 1, MR * N) as at:
                        for u in range(MR):
                            first = sp.compute_val(at + (u * N + HALF * half))
                            sp.wait_ge(S["f_t"], at // N + half * NB + u + 1)
                            sp.dma_start(mring[:, u], maskT[:, bass.ds(first, HALF)]).then_inc(
                                S[f"f_mask{u}"], 16)

            for l in range(LAYERS):
                S = L[l]
                branch(sp, l, general, fast)
                sp.wait_ge(S["left"], 4)
                for n in path.values():
                    sp.sem_clear(n)
                sp.drain().then_inc(S["go"], 1)
            sp.wait_ge(L[LAYERS - 1]["layer"], 1)
            sp.dma_start(out_v, h[dst(LAYERS - 1)][:, :, 0:F]).then_inc(out_ready, 16)
            sp.wait_ge(out_ready, 16)

        @block.gpsimd
        def _(pool):
            nc.gpsimd.memset(identf[:], 0.0).then_inc(consts, 1)
            pool.wait_ge(consts, 1)
            nc.gpsimd.affine_select(out=identf[:], in_=identf[:], compare_op=ALU.not_equal, fill=1.0, base=0,
                                    pattern=[[-1, P]], channel_multiplier=1).then_inc(consts, 1)

            def general(l):
                S = L[l]

                def load(s, half):
                    for k in range(SB):
                        pool.dma_start(nat[:, half, k, :], adj_v[s * SB + k]).then_inc(
                            S[f"landed{half * SB + k}"], 16)

                load(0, 0)
                with pool.Fori(0, NS // 2) as J:
                    pool.wait_ge(S["turned"], J * 2 * NB + NB)
                    load(J * 2 + 1, 1)
                    pool.wait_ge(S["turned"], J * 2 * NB + 2 * NB)
                    load((J * 2 + 2) % NS, 0)

            def fast(l):
                S = L[l]
                pool.wait_ge(S["f_exp"], 2)
                nc.gpsimd.tensor_tensor(VW[:, :, 0:F - 1], h[src(l)][:, :, 0:F - 1],
                                        wcol[:, :].unsqueeze(2).to_broadcast([P, NB, F - 1]),
                                        ALU.mult).then_inc(S["f_vw"], 1)

            for l in range(LAYERS):
                S = L[l]
                pool.wait_ge(S["ext_ready"], 1)
                nc.gpsimd.partition_all_reduce(exta[:, 0:2], ext[:, 0:2], P, RMAX).then_inc(S["ext_all"], 1)
                branch(pool, l, general, fast)
                pool.drain().then_inc(S["left"], 1)

        @block.tensor
        def _(pe):
            pe.wait_ge(setup_dve, 1)
            for m in range(2):
                nc.tensor.matmul(rowp[0][0:F, F * m:F * m + F], wmat[:, m, :], identf[0:F, 0:F],
                                 start=True, stop=True).then_inc(setup_pe, 1)
            for l in range(LAYERS):
                for t in range(2):
                    n = 2 * l + t
                    pe.wait_ge(setup_dve, 2 + n)
                    rhs = wt[:, l, :] if l < 2 else identf[0:F, 0:F]
                    nc.tensor.matmul(rowp[1][:, 0:F], arep[:, :], rhs, start=True, stop=True).then_inc(setup_pe, 1)
            pe.wait_ge(setup_dve, 2 + 2 * LAYERS)
            for m in range(2):
                nc.tensor.matmul(rowp[0][:, F * m:F * m + F], MT[:, :], wmat[:, 1, :] if m else identf[0:F, 0:F],
                                 start=True, stop=True).then_inc(setup_pe, 1)

            def colsums(l):
                S = L[l]
                V = h[src(l)]
                e = E[:, 1 if l == 1 else 0, :]
                for b in range(NB):
                    mm = nc.tensor.matmul(natp[0:F1, 0:P], V[:, b, :], onesf[:, :], start=(b == 0), stop=(b == NB - 1))
                mm.then_inc(S["cs_mm"], 1)
                pe.wait_ge(S["cs_ok"], 1)
                nc.tensor.matmul(natp[:, 0:F1], colsum[:, :], e, start=True, stop=True).then_inc(S["mr_mm"], 1)

            def fast(l):
                S = L[l]
                e = 1 if l == 1 else 0

                def rows(c):
                    pe.wait_ge(S["f_diag"], c + 1)
                    if c >= 2:
                        pe.wait_ge(S["f_row"], c - 1)
                    nc.tensor.matmul(rowp[c % 2][:, :], onesf[:, :], diag[:, c % 2], start=True,
                                     stop=True).then_inc(S["f_rmm"], 1)

                def tile(half, b):
                    n = half * NB + b
                    pe.wait_ge(S["f_t"], MR + n + 1)
                    for c in range(SB):
                        a = F * (c % 2)
                        mm = nc.tensor.matmul(Wp[2 * half + c // 2][a:a + F, :], VW[:, b, :],
                                              T[:, n % TR, CW * c:CW * c + CW], start=(b == 0), stop=(b == NB - 1))
                    mm.then_inc(S["f_pv"], 1)

                def natural(half):
                    pe.wait_ge(S["f_num"], 2 * half + 2)
                    for c in range(SB):
                        if c >= 2 or half:
                            pe.wait_ge(S["f_nat"], SB * half + c - 1)
                        a = F * (c % 2)
                        for k in range(SB):
                            at = CW * (c // 2) + P * k
                            mm = nc.tensor.matmul((natp, acc)[c % 2][:, F1 * k:F1 * k + F1],
                                                  numF[a:a + F, at:at + P], EF[a:a + F, e, :], start=True, stop=True)
                        mm.then_inc(S["nat_mm"], 1)

                for c in range(4):
                    rows(c)
                pe.wait_ge(S["f_vw"], 2)
                pe.sem_inc(S["f_pv"], TR)
                for b in range(NB):
                    tile(0, b)
                    if b in ROWS_AT:
                        rows(SB + ROWS_AT.index(b))
                    if b == 26:
                        colsums(l)
                for b in range(NB):
                    tile(1, b)
                    if b == 4:
                        pe.wait_ge(S["mr_ok"], 1)
                        natural(0)
                natural(1)

            def general(l):
                S = L[l]
                V = h[src(l)]
                e = E[:, 1 if l == 1 else 0, :]
                pe.sem_inc(S["turned"], NB)
                colsums(l)
                for c in range(N // CW):
                    pe.wait_ge(S["diag_d"], c + 1)
                    if c >= 2:
                        pe.wait_ge(S["drow_ok"], c - 1)
                    nc.tensor.matmul(rowp[c % 2][:, :], onesf[:, :], diag[:, c % 2], start=True, stop=True).then_inc(
                        S["drow_mm"], 1)
                with pe.Fori(0, NS // 2) as J:
                    for half in range(2):
                        s = J * 2 + half
                        pe.wait_ge(S["diag_ok"], s + 1)
                        for q in range(2):
                            mm = nc.tensor.matmul(rowp[q][:, :], onesf[:, :], diag[:, q], start=True, stop=True)
                        mm.then_inc(S["rows_mm"], 1)
                        pe.wait_ge(S["binned"], s * SB + SB)
                        for t in range(NB + 3):
                            if t < NB:
                                for k in range(SB):
                                    mm = nc.tensor.matmul(Wp[t % RING][:, P * k:P * k + P], nat_j[:, half, k, t, :],
                                                          identb[:, :], start=(k == 0), stop=True,
                                                          skip_group_check=True)
                                mm.then_inc(S["turned"], 1)
                            if 0 <= t - 1 < NB:
                                if t == 1:
                                    pe.wait_ge(S["rows_ok"], s + 1)
                                pe.wait_ge(S["saved"], (s * NB + t) * (CW // NB))
                                nc.tensor.matmul(Wp[(t - 1) % RING][:, :], picks[:, :], s2rows[:, :], start=False,
                                                 stop=True, skip_group_check=True).then_inc(S["w_full"], 1)
                            if 0 <= t - 3 < NB:
                                b = t - 3
                                pe.wait_ge(S["p_full"], s * NB + b + 1)
                                mm = nc.tensor.matmul(acc[0:F1, :], V[:, b, :], U[:, b % RING, :], start=(b == 0),
                                                      stop=(b == NB - 1))
                        mm.then_inc(S["acc_full"], 1)
                        pe.wait_ge(S["numt_ok"], s + 1)
                        for k in range(SB):
                            mm = nc.tensor.matmul(natp[:, F1 * k:F1 * k + F1], numT[:, P * k:P * k + P], e,
                                                  start=True, stop=True)
                        mm.then_inc(S["nat_mm"], 1)

            for l in range(LAYERS):
                pe.wait_ge(hready, l + 1)
                branch(pe, l, general, fast)
                pe.drain().then_inc(L[l]["left"], 1)

        @block.scalar
        def _(act):
            def colsums(l):
                S = L[l]
                act.wait_ge(S["cs_mm"], 1)
                nc.scalar.activation(colsum[:, :], natp[0:F1, 0:P], ACT.Copy).then_inc(S["cs_ok"], 1)
                act.wait_ge(S["mr_mm"], 1)
                nc.scalar.activation(meanrow[:, :], natp[:, 0:F1], ACT.Copy).then_inc(S["mr_ok"], 1)

            def fast(l):
                S = L[l]
                act.wait_ge(S["f_in"], 1)
                nc.scalar.activation(qcol[:, :], st[:, 0, :], ACT.Exp, scale=1.0 - SLOPE[l]).then_inc(S["f_exp"], 1)
                nc.scalar.activation(wcol[:, :], st[:, 0, :], ACT.Exp, scale=SLOPE[l]).then_inc(S["f_exp"], 1)
                nc.scalar.activation(rcol[:, :], st[:, 1, :], ACT.Exp, scale=SLOPE[l] - 1.0).then_inc(S["f_exp"], 1)
                act.wait_ge(S["f_exp"], 2)
                nc.scalar.activation(VW[:, :, F - 1:F], wcol[:, :].unsqueeze(2), ACT.Copy).then_inc(S["f_vw"], 1)

                def rows(c):
                    act.wait_ge(S["f_rmm"], c + 1)
                    nc.scalar.activation(drow[:, CW * c:CW * c + CW], rowp[c % 2][:, :], ACT.Copy).then_inc(
                        S["f_row"], 1)

                for c in range(8):
                    rows(c)
                colsums(l)
                for half in range(2):
                    act.wait_ge(S["f_pv"], TR + NB * (half + 1))
                    for b in range(2):
                        nc.scalar.activation(numF[:, CW * b:CW * b + CW], Wp[2 * half + b][:, :],
                                             ACT.Copy).then_inc(S["f_num"], 1)
                    for c in range(SB):
                        act.wait_ge(S["nat_mm"], SB * half + c + 1)
                        s0 = SB * (SB * half + c)
                        nc.scalar.activation(agg[:, s0:s0 + SB, :], (natp, acc)[c % 2][:, 0:SB * F1].rearrange(
                            "p (k f) -> p k f", k=SB), ACT.Copy).then_inc(S["f_nat"], 1)
                        if c == SB - 1:
                            act.wait_ge(S["f_nat"], SB * half + SB)
                act.sem_inc(S["agg_ok"], NS)

            def general(l):
                S = L[l]
                colsums(l)
                for c in range(N // CW):
                    act.wait_ge(S["drow_mm"], c + 1)
                    nc.scalar.activation(drow_b[:, SB * c:SB * c + SB, :],
                                         rowp[c % 2][:, :].rearrange("p (b j) -> p b j", b=SB), ACT.Copy).then_inc(
                        S["drow_ok"], 1)
                with act.Fori(0, NS // 2) as J:
                    for half in range(2):
                        s = J * 2 + half
                        act.wait_ge(S[f"stored{half}"], 16 * J + 16)
                        act.wait_ge(S["rows_mm"], s + 1)
                        nc.scalar.activation(s2hi[:, :], rowp[0][0:65, :], ACT.Copy).then_inc(S["rows_ev"], 1)
                        nc.scalar.activation(s2rows[0:1, :], rowp[0][0:1, :], ACT.Copy).then_inc(S["rows_ev"], 1)
                        nc.scalar.activation(xrow[:, :], rowp[1][:, :], ACT.Copy).then_inc(S["rows_ev"], 1)
                        for t in range(NB + 2):
                            if t < NB:
                                act.wait_ge(S["turned"], s * NB + t + 1 + NB)
                                nc.scalar.activation(stg[:, half, t, :], Wp[t % RING][:, :], ACT.Relu,
                                                     bias=1.0).then_inc(S["saved"], CW // NB)
                            if t >= 2:
                                b = t - 2
                                act.wait_ge(S["u_full"], s * NB + b + 1)
                                nc.scalar.activation(U[:, b % RING, :], U[:, b % RING, :], ACT.Exp,
                                                     bias=dcol[:, b:b + 1]).then_inc(S["p_full"], 1)
                        act.wait_ge(S["acc_full"], s + 1)
                        nc.scalar.activation(numT[:, :], acc[0:F1, :], ACT.Copy).then_inc(S["numt_ok"], 1)
                        act.wait_ge(S["nat_mm"], s + 1)
                        nc.scalar.activation(agg[:, bass.ts(s, SB), :],
                                             natp[:, 0:SB * F1].rearrange("p (k f) -> p k f", k=SB),
                                             ACT.Copy).then_inc(S["agg_ok"], 1)

            for l in range(LAYERS):
                S = L[l]
                branch(act, l, general, fast)
                act.drain().then_inc(S["left"], 1)
                if OUTPUT[l] == ELU:
                    act.wait_ge(S["elu_in"], 1)
                    nc.scalar.activation(tmp[:, :, 0:F], tmp[:, :, 0:F], ACT.Exp).then_inc(S["elu_out"], 1)

        @block.vector
        def _(dve):
            v = nc.vector

            def then_drain(_):
                dve.drain()

            def rows_of(col, n):
                return col.unsqueeze(2).to_broadcast([P, n, F])

            def scores(l):
                for t, (node, col) in enumerate(((h[res(l)], scol), (h[src(l)], dcol))):
                    v.tensor_tensor(tmp[:, :, 0:F], node[:, :, 0:F],
                                    wrow[:, l, t, :].unsqueeze(1).to_broadcast([P, NB, F]), ALU.mult)
                    dve.drain()
                    v.tensor_reduce(col[:, :], tmp[:, :, 0:F], AX.X, ALU.add)
                    dve.drain()
                v.tensor_scalar(ycol[:, :], dcol[:, :], -(1.0 - SLOPE[l]), None, ALU.mult)
                v.tensor_reduce(ext[:, 0:1], dcol[:, :], AX.X, ALU.max)
                v.tensor_reduce(ext[:, 1:2], dcol[:, :], AX.X, ALU.min, negate=True)
                dve.drain().then_inc(L[l]["ext_ready"], 1)

            v.memset(onesf[:], 1.0)
            v.memset(picks[:], 0.0)
            v.memset(s2rows[:], 0.0)
            for b in range(2):
                v.memset(h[b][:, :, F:F1], 1.0)
            dve.drain()
            for r in (0, 32, 64):
                v.memset(picks[r:r + 1, :], 1.0)
            dve.wait_ge(consts, 2)
            v.tensor_copy(identb[:], identf[:])
            dve.wait_ge(loaded, 16 * 12)
            for m in range(2):
                v.tensor_copy(E[:, m, :], identf[0:F1, 0:F1])
            dve.drain()
            v.tensor_copy(E[0:F, 1, 0:F], wmat[:, 1, :])
            dve.drain().then_inc(setup_dve, 1)
            dve.wait_ge(setup_pe, 2)
            v.tensor_copy(wt[:, :, :], rowp[0][0:F, 0:2 * F].rearrange("p (m f) -> p m f", m=2))
            for l in range(LAYERS):
                for t in range(2):
                    n = 2 * l + t
                    v.tensor_scalar(arep[:, :], onesf[0:F, :], acol[:, l, t:t + 1], None, ALU.mult)
                    dve.drain().then_inc(setup_dve, 1)
                    dve.wait_ge(setup_pe, 3 + n)
                    v.tensor_copy(wrow[:, l, t, :], rowp[1][:, 0:F])
                    dve.drain()
            last = identf[0:F, F - 1:F]
            for q in range(2):
                v.tensor_scalar(MT[:, F * q:F * q + F - 1], identf[0:F, 0:F - 1], last, None, ALU.subtract)
                v.memset(MT[:, F * q + F - 1:F * q + F], 0.0)
            dve.drain().then_inc(setup_dve, 1)
            dve.wait_ge(setup_pe, 2 + 2 * LAYERS + 2)
            v.tensor_copy(EF[:, :, 0:F], rowp[0][:, 0:2 * F].rearrange("p (m f) -> p m f", m=2))
            for m in range(2):
                v.tensor_tensor(EF[:, m, F:F1], identf[:, F - 1:F], identf[:, P - 1:P], ALU.add)
            scores(0)
            dve.drain().then_inc(hready, 1)

            def bounds(l):
                S = L[l]
                dve.wait_ge(S["ext_all"], 1)
                v.tensor_tensor(ext[:, 2:3], exta[:, 0:1], exta[:, 1:2], ALU.add)
                dve.drain()
                if l:
                    v.tensor_scalar(choice[:, :], ext[:, 2:3], FAST_RANGE, None, ALU.is_le)
                    dve.drain().then_inc(S["choice"], 1)

            def fast(l):
                S = L[l]
                v.tensor_scalar(st[:, 0, :], dcol[:, :], exta[:, 0:1], None, ALU.subtract)
                v.tensor_scalar(st[:, 1, :], scol[:, :], exta[:, 0:1], 0.0, ALU.add, ALU.max)
                dve.drain().then_inc(S["f_in"], 1)
                dve.wait_ge(S["f_exp"], 3)

                def rows(c):
                    if c >= 2:
                        dve.wait_ge(S["f_rmm"], c - 1)
                    v.tensor_tensor(diag[:, c % 2], identf[:, :].unsqueeze(1).to_broadcast([P, SB, P]),
                                    rcol[:, SB * c:SB * c + SB].unsqueeze(2).to_broadcast([P, SB, P]),
                                    ALU.mult).then_inc(S["f_diag"], 1)

                def tiles(half, g0, g1):
                    with dve.Fori(g0, g1) as g:
                        for u in range(MR):
                            n = half * NB + u
                            dve.wait_ge(S[f"f_mask{u}"], g * 16 + 16 * (half * (NB // MR) + 1))
                            dve.wait_ge(S["f_pv"], g * MR + n + 1)
                            v.scalar_tensor_tensor(
                                out=T[:, u % TR, :], in0=drow[:, HALF * half:HALF * half + HALF],
                                scalar=qcol[:, bass.ds(g * MR + u, 1)], in1=mring[:, u, :],
                                op0=ALU.max, op1=ALU.mult).then_inc(S["f_t"], 1)

                dve.sem_inc(S["f_t"], MR)
                for c in range(SB + 2):
                    rows(c)
                dve.wait_ge(S["f_row"], SB)
                tiles(0, 0, 1)
                rows(6)
                tiles(0, 1, 2)
                rows(7)
                tiles(0, 2, NB // MR)
                dve.wait_ge(S["f_row"], 2 * SB)
                tiles(1, 0, NB // MR)

            def general(l):
                S = L[l]
                slope = SLOPE[l]
                for c in range(NB // SB):
                    if c >= 2:
                        dve.wait_ge(S["drow_mm"], c - 1)
                    v.tensor_tensor(diag[:, c % 2], identf[:, :].unsqueeze(1).to_broadcast([P, SB, P]),
                                    dcol[:, SB * c:SB * c + SB].unsqueeze(2).to_broadcast([P, SB, P]),
                                    ALU.mult).then_inc(S["diag_d"], 1)
                v.tensor_scalar(ext[:, 3:4], ext[:, 2:3], -2.0, -256.0, ALU.mult, ALU.add)
                v.tensor_scalar(exta[:, 2:3], exta[:, 1:2], -1.0, None, ALU.mult)
                dve.drain()
                dve.wait_ge(S["drow_ok"], N // CW)
                dve.wait_ge(S["drow_mm"], N // CW)

                def binarise(half, k, turn):
                    dve.wait_ge(S[f"landed{half * SB + k}"], turn)
                    v.tensor_scalar(nat[:, half, k, :], nat[:, half, k, :], 0.0, ext[:, 3:4], ALU.is_le, ALU.mult)
                    dve.drain().then_inc(S["binned"], 1)

                def row_max(half, k, c):
                    dve.drain()
                    v.tensor_tensor_reduce(junk[:, :], nat[:, half, k, CHUNK * c:CHUNK * c + CHUNK],
                                           drow[:, CHUNK * c:CHUNK * c + CHUNK], 1.0, -3.0e38, ALU.add, ALU.max,
                                           rmax[:, k, c:c + 1])

                def row_terms(s):
                    dve.drain()
                    v.tensor_reduce(sm[:, 0, :], rmax[:, :, :], AX.X, ALU.max)
                    dve.drain()
                    v.tensor_scalar(sm[:, 1, :], sm[:, 0, :], exta[:, 2:3], None, ALU.max)
                    dve.drain()
                    sc = scol[:, bass.ts(s, SB)]
                    v.tensor_tensor(sm[:, 2, :], sm[:, 1, :], sc, ALU.add)
                    dve.drain()
                    v.scalar_tensor_tensor(out=sm[:, 3, :], in0=sm[:, 2, :], scalar=slope, in1=sm[:, 2, :],
                                           op0=ALU.mult, op1=ALU.max)
                    dve.drain()
                    v.scalar_tensor_tensor(out=sm[:, 4, :], in0=sc, scalar=slope, in1=sm[:, 3, :],
                                           op0=ALU.mult, op1=ALU.subtract)
                    v.tensor_scalar(sm[:, 5, :], sc, 1.0 - slope, None, ALU.mult)
                    dve.drain()
                    v.tensor_tensor(diag[:, :, :, :].rearrange("p q k j -> p (q k) j"),
                                    identf[:, :].unsqueeze(1).to_broadcast([P, 2 * SB, P]),
                                    sm[:, 4:6, :].rearrange("p q k -> p (q k)").unsqueeze(2).to_broadcast(
                                        [P, 2 * SB, P]), ALU.mult).then_inc(S["diag_ok"], 1)

                for k in range(SB):
                    binarise(0, k, 16)
                    for c in range(NCH):
                        row_max(0, k, c)
                row_terms(0)
                with dve.Fori(0, NS // 2) as J:
                    for half in range(2):
                        s = J * 2 + half
                        dve.wait_ge(S["rows_ev"], 3 * s + 3)
                        v.tensor_tensor(s2r[:, :], rowp[0][0:65, :], s2hi[:, :], ALU.subtract)
                        dve.drain()
                        v.tensor_copy(s2mid[:, :], s2r[:, :])
                        dve.drain()
                        v.tensor_copy(s2rows[32:33, :], s2mid[32:33, :])
                        v.tensor_tensor(s2rows[64:65, :], s2r[64:65, :], s2mid[64:65, :], ALU.subtract)
                        dve.drain().then_inc(S["rows_ok"], 1)
                        for t in range(NB):
                            dve.wait_ge(S["w_full"], s * NB + t + 1)
                            v.scalar_tensor_tensor(out=U[:, t % RING, :], in0=xrow[:, :], scalar=ycol[:, t:t + 1],
                                                   in1=Wp[t % RING][:, :], op0=ALU.max,
                                                   op1=ALU.add).then_inc(S["u_full"], 1)
                            if t % 8 == 0:
                                binarise(1 - half, t // 8, 16 * J + (16 if half == 0 else 32))
                            if t % 2 == 1:
                                row_max(1 - half, t // 8, t % 8 // 2)
                        row_terms((s + 1) % NS)

            for l in range(LAYERS):
                S = L[l]
                bounds(l)
                branch(dve, l, general, fast)
                dve.wait_ge(S["agg_ok"], NS)
                dve.wait_ge(S["mr_ok"], 1)
                dve.drain().then_inc(S["left"], 1)
                den = agg[:, :, F:F1].rearrange("p b o -> p (b o)")
                v.tensor_scalar(st[:, 0, :], den, 0.0, None, ALU.is_le)
                dve.drain()
                v.tensor_tensor(tmp[:, :, :], st[:, 0, :].unsqueeze(2).to_broadcast([P, NB, F1]),
                                meanrow[:, :].unsqueeze(1).to_broadcast([P, NB, F1]), ALU.mult)
                dve.drain()
                v.tensor_tensor(agg[:, :, :], agg[:, :, :], tmp[:, :, :], ALU.add)
                dve.drain()
                v.reciprocal(st[:, 1, :], den)
                dve.drain()
                A = agg[:, :, 0:F]
                Z = tmp[:, :, 0:F]
                H = h[res(l)][:, :, 0:F]
                v.tensor_tensor(A, A, rows_of(st[:, 1, :], NB), ALU.mult)
                dve.drain()
                if l == 0:
                    v.tensor_tensor(A, A, H, ALU.add)
                    dve.drain()
                if OUTPUT[l] == ELU:
                    v.tensor_scalar(Z, A, 0.0, None, ALU.min)
                    dve.drain().then_inc(S["elu_in"], 1)
                    dve.wait_ge(S["elu_out"], 1)
                    v.scalar_tensor_tensor(out=A, in0=A, scalar=0.0, in1=Z, op0=ALU.max, op1=ALU.add)
                    dve.drain()
                    v.scalar_tensor_tensor(out=A, in0=A, scalar=-1.0, in1=H, op0=ALU.add, op1=ALU.add)
                elif OUTPUT[l] == RELU:
                    v.scalar_tensor_tensor(out=A, in0=A, scalar=0.0, in1=H, op0=ALU.max, op1=ALU.add)
                else:
                    v.tensor_tensor(A, A, H, ALU.add)
                dve.drain()
                v.tensor_reduce(st[:, 2, :], A, AX.X, ALU.add)
                dve.drain()
                v.tensor_scalar(st[:, 3, :], st[:, 2, :], 1.0 / F, None, ALU.mult)
                dve.drain()
                v.tensor_tensor(A, A, rows_of(st[:, 3, :], NB), ALU.subtract)
                dve.drain()
                v.tensor_tensor(Z, A, A, ALU.mult)
                dve.drain()
                v.tensor_reduce(st[:, 4, :], Z, AX.X, ALU.add)
                dve.drain()
                v.tensor_scalar(st[:, 5, :], st[:, 4, :], 1.0 / F, EPS, ALU.mult, ALU.add)
                dve.drain()
                v.tensor_scalar(st[:, 6, :].bitcast(I32), st[:, 5, :].bitcast(I32), 1, None,
                                ALU.logical_shift_right)
                dve.drain()
                v.tensor_scalar(st[:, 7, :].bitcast(I32), st[:, 6, :].bitcast(I32), -1.0, MAGIC, ALU.mult, ALU.add)
                dve.drain()
                for _ in range(4):
                    v.tensor_tensor(st[:, 6, :], st[:, 7, :], st[:, 7, :], ALU.mult)
                    dve.drain()
                    v.scalar_tensor_tensor(out=st[:, 6, :], in0=st[:, 6, :], scalar=-0.5, in1=st[:, 5, :],
                                           op0=ALU.mult, op1=ALU.mult)
                    dve.drain()
                    v.scalar_tensor_tensor(out=st[:, 7, :], in0=st[:, 6, :], scalar=1.5, in1=st[:, 7, :],
                                           op0=ALU.add, op1=ALU.mult)
                    dve.drain()
                v.tensor_tensor(h[dst(l)][:, :, 0:F], A, rows_of(st[:, 7, :], NB), ALU.mult)
                dve.drain().then_inc(S["layer"], 1)
                if l + 1 < LAYERS:
                    scores(l + 1)
                    dve.drain().then_inc(hready, 1)


_INS = ["x", "adj", "L0_gnn_entity_embs", "L0_gnn_W", "L0_gnn_a", "L1_gnn_W", "L1_gnn_a", "L2_gnn_a", "L3_gnn_a"]


def kernel(**inputs):
    import numpy as _np
    import concourse.bacc as _bacc
    from concourse import mybir as _mybir
    from concourse.bass_utils import run_bass_kernel_spmd as _run

    nc = _bacc.Bacc("TRN2", target_bir_lowering=False, num_devices=1)
    arrays, args = {}, []
    for name in _INS:
        a = _np.ascontiguousarray(inputs[name])
        arrays[f"in_{name}_dram"] = a
        args.append(nc.dram_tensor(f"in_{name}_dram", a.shape, _mybir.dt.from_np(a.dtype), kind="ExternalInput").ap())
    shape = inputs["x"].shape
    res = nc.dram_tensor("out_dram", shape, _mybir.dt.float32, kind="ExternalOutput").ap()
    build(nc, *args, res)
    r = _run(nc, [arrays], core_ids=[0])
    return r.results[0]["out_dram"]
```

```python
from contextlib import ExitStack

import concourse.bass as bass
from concourse import mybir

ALU = mybir.AluOpType
ACT = mybir.ActivationFunctionType
AX = mybir.AxisListType
F32 = mybir.dt.float32
BF16 = mybir.dt.bfloat16
U8 = mybir.dt.uint8
I32 = mybir.dt.int32
RMAX = bass.bass_isa.ReduceOp.max

P = 128
SLOPE = (0.2, 0.2, 0.01, 0.2)
ELU, NONE, RELU = "elu", "none", "relu"
OUTPUT = (ELU, ELU, NONE, RELU)
EPS = 1e-5
MAX_BOUND = 32.0
DVE_AT = ((1, 4, 8, 11, 13), (5, 10, 14, 16, 18), (5, 9, 13, 16, 18), (5, 8, 12, 15, 18))
NATURAL_AT = 1
ROWS_AT = (24, 25, 26, 27)
LOOP_AT = 20
TERMS_AT, PRODUCTS_AT, EVACUATE_AT, SPLIT_AT = 24, 28, 29, 29
ALONE_EXP_AT = 12
HOOKS0 = (2, 5, 12, 17, 22, 26, 29)
LAGS = (7,) * 10 + (6,) * 4 + (5,) * 14 + (6, 6, 7, 7)
LAST_LAGS = (7,) * 10 + (6,) * 4 + (5,) * 4 + (4,) * 14
LAG = 7
SUMS_AT, TURN_AT, TURNED_AT = 8, 10, 12
MAGIC = float(0x5F3759DF)


def build(nc, x, adj, ent, W0, a0, W1, a1, a2, a3, out):
    N, F = x.shape
    NB = N // P
    SB = 4
    NS = NB // SB
    CW = SB * P
    F1 = F + 1
    RING = 4
    URING = 8
    CHUNK = 2048
    NCH = N // CHUNK
    LAYERS = 4
    HALF = N // 2
    TR = 4
    MR = 4
    STEPS = 2 * (LAYERS - 1)
    HB = NB // 2

    ctx = ExitStack()
    with ctx:
        def sb(name, shape, dt):
            return ctx.enter_context(nc.sbuf_tensor(name, shape, dt))

        def ps(name):
            return ctx.enter_context(nc.psum_tensor(name, [P, 512], F32))

        def sem(name):
            return ctx.enter_context(nc.semaphore(name))

        h = [sb("h0", [P, NB, F1], F32), sb("h1", [P, NB, F1], F32)]
        agg = sb("agg", [P, NB, F1], F32)
        tmp = sb("tmp", [P, NB, F1], F32)
        identf = sb("identf", [P, P], F32)
        negb = sb("negb", [P, P], BF16)
        onesf = sb("onesf", [P, P], F32)
        picks = sb("picks", [65, P], BF16)
        wmat = sb("wmat", [F, 2, F], F32)
        acol = sb("acol", [F, LAYERS, 2], F32)
        arep = sb("arep", [F, 2 * LAYERS, P], F32)
        wt = sb("wt", [F, 2, F], F32)
        wrow = sb("wrow", [P, LAYERS, 2, F], F32)
        E = sb("E", [F1, 2, F1], F32)
        colsum = sb("colsum", [F1, P], F32)
        meanrow = sb("meanrow", [P, F1], F32)
        scol = sb("scol", [P, NB], F32)
        dcol = sb("dcol", [P, NB], F32)
        ycol = sb("ycol", [P, NB], F32)
        st = sb("st", [P, 8, NB], F32)
        ext = sb("ext", [P, 4], F32)
        exta = sb("exta", [P, 4], F32)
        drow = sb("drow", [P, N], F32)
        nat = sb("nat", [P, 2, SB, N], BF16)
        junk = sb("junk", [P, CHUNK], BF16)
        rmax = sb("rmax", [P, SB, NCH], F32)
        sm = sb("sm", [P, 8, SB], F32)
        diag = sb("diag", [P, 4, SB, P], F32)
        xrow = sb("xrow", [P, 2, CW], F32)
        s2hi = sb("s2hi", [65, 2, CW], BF16)
        s2r = sb("s2r", [65, CW], F32)
        s2mid = sb("s2mid", [65, CW], BF16)
        s2rows = sb("s2rows", [65, 2, CW], BF16)
        U = sb("U", [P, URING, CW], F32)
        stg = sb("stg", [P, 2, NB, CW], U8)
        numT = sb("numT", [F1, CW], F32)
        numF = sb("numF", [P, 2 * CW], F32)
        choice = sb("choice", [P, 1], I32)
        qcol = sb("qcol", [P, 2, NB], F32)
        fst = sb("fst", [P, 10, NB], F32)
        bound = sb("bound", [P, 6, LAYERS - 1], F32)
        eps = sb("eps", [P, 1], F32)
        dless = sb("dless", [P, NB], F32)
        wcol = sb("wcol", [P, NB], F32)
        rcol = sb("rcol", [P, NB], F32)
        VW = [nat[:, 1, k].bitcast(F32).rearrange("p (b f) -> p b f", f=F) for k in range(2)]
        MT = sb("MT", [F, 2 * F], F32)
        EF = sb("EF", [P, 2, F1], F32)
        T = nat[:, 0].rearrange("p k j -> p (k j)").bitcast(F32).rearrange("p (t i) -> p t i", t=TR)
        mring = stg[:, 0].rearrange("p b i -> p (b i)").rearrange("p (t i) -> p t i", i=HALF)

        Wp = [ps(f"Wp{i}") for i in range(RING)]
        rowp = [ps("rowp0"), ps("rowp1")]
        accp = [ps("accp0"), ps("accp1")]

        maskT = nc.dram_tensor("maskT", [P, NB * N], U8, kind="Internal").ap()

        loaded = sem("loaded")
        entities_loaded = sem("entities_loaded")
        x_loaded = sem("x_loaded")
        consts = sem("consts")
        setup_pe = sem("setup_pe")
        setup_dve = sem("setup_dve")
        hready = sem("hready")
        out_ready = sem("out_ready")

        adj_v = adj.rearrange("(p b) j -> b p j", b=NB)
        nat_j = nat[:, :, :, :].rearrange("p h k (j b) -> p h k b j", b=NB)
        drow_b = drow[:, :].rearrange("p (j b) -> p b j", b=NB)
        x_v = x.rearrange("(p b) f -> p b f", b=NB)
        ent_v = ent.rearrange("(p b) f -> p b f", b=NB)
        out_v = out.rearrange("(p b) f -> p b f", b=NB)
        mask_v = maskT.rearrange("p (b i) -> p b i", b=NB)

        path = {n: sem(n) for n in (
            "diag_d", "drow_mm", "drow_ok", "cs_mm", "cs_ok", "mr_mm", "mr_ok",
            "binned", "diag_ok", "rows_mm", "rows_ev", "rows_ok", "turned", "saved", "stored0", "stored1",
            "w_full", "u_full", "p_full", "acc_full", "numt_ok", "nat_mm", "agg_ok")}
        L = [path | {n: sem(f"{n}_{l}") for n in (
            "ext_ready", "ext_all", "elu_in", "elu_out", "left", "go") + tuple(
                f"landed{i}" for i in range(2 * SB))} for l in range(LAYERS)]

        C = {n: sem(n) for n in (
            "flags", "flags_all", "choice", "recips", "summed", "scaled", "activated", "squared", "normed",
            "d_ready", "q_ready", "w_ready", "vw_ready", "s_ready", "r_ready", "diags", "row_mm", "row_ok",
            "tiles", "used", "num_ok", "turned_mm", "turned_ok", "half_out") + tuple(
                f"mask{i}" for i in range(MR))}

        block = ctx.enter_context(nc.Block())

        def src(l):
            return 1 if l == 0 else (l + 1) % 2

        def res(l):
            return 0 if l == 0 else (l + 1) % 2

        def dst(l):
            return 0 if l == 0 else l % 2

        def parts(f):
            return f // 2, f % 2

        def branch(eng, fast, general):
            eng.wait_ge(C["choice"], 1)
            bounded = eng.value_load(choice[0:1, 0:1], min_val=0, max_val=1)
            with eng.If(bounded):
                fast()
            with eng.Else():
                if eng is not nc.sync:
                    eng.wait_ge(L[0]["go"], 1)
                    eng.drain()
                general()

        @block.sync
        def _(sp):
            sp.dma_start(wmat[:, 0, :], W0).then_inc(loaded, 16)
            for l, a in enumerate((a0, a1, a2, a3)):
                sp.dma_start(acol[:, l, :], a.rearrange("(t f) o -> f (t o)", t=2),
                             allow_slow_non_contiguous=True).then_inc(loaded, 16)
            sp.dma_start(wmat[:, 1, :], W1).then_inc(loaded, 16)
            sp.dma_start(h[1][:, :, 0:F], ent_v).then_inc(entities_loaded, 16)
            sp.dma_start(h[0][:, :, 0:F], x_v).then_inc(x_loaded, 16)

            def general(l):
                S = L[l]
                for half in range(2):
                    sp.sem_inc(S[f"stored{half}"], 16)
                with sp.Fori(0, N - 2 * CW + 1, 2 * CW) as i0:
                    for half in range(2):
                        sp.wait_ge(S["saved"], i0 + (half + 1) * CW)
                        sp.dma_start(mask_v[:, :, bass.ds(i0 + half * CW, CW)], stg[:, half]).then_inc(
                            S[f"stored{half}"], 16)
                for half in range(2):
                    sp.wait_ge(S[f"stored{half}"], 16 + 16 * NS // 2)

            def clear(l):
                sp.wait_ge(L[l]["left"], 4)
                for n in path.values():
                    sp.sem_clear(n)
                sp.drain().then_inc(L[l]["go"], 1)

            def fast():
                for g in range(STEPS):
                    half = g % 2
                    with sp.Fori(0 if g else MR * N, NB * N - MR * N + 1, MR * N) as at:
                        for u in range(MR):
                            first = sp.compute_val(at + (u * N + HALF * half))
                            sp.wait_ge(C["tiles"], at // N + g * NB + u + 1)
                            sp.dma_start(mring[:, u], maskT[:, bass.ds(first, HALF)]).then_inc(
                                C[f"mask{u}"], 16)

            def others():
                for u in range(MR):
                    sp.wait_ge(C[f"mask{u}"], 16)
                clear(0)
                for l in range(1, LAYERS):
                    general(l)
                    clear(l)

            general(0)
            for u in range(MR):
                sp.dma_start(mring[:, u], maskT[:, u * N:u * N + HALF]).then_inc(C[f"mask{u}"], 16)
            branch(sp, fast, others)
            for half in range(2):
                sp.wait_ge(C["half_out"], half + 1)
                b = slice(HB * half, HB * half + HB)
                sp.dma_start(out_v[:, b], h[dst(LAYERS - 1)][:, b, 0:F]).then_inc(out_ready, 16)
            sp.wait_ge(out_ready, 32)

        @block.gpsimd
        def _(pool):
            nc.gpsimd.memset(identf[:], 0.0).then_inc(consts, 1)
            pool.wait_ge(consts, 1)
            nc.gpsimd.affine_select(out=identf[:], in_=identf[:], compare_op=ALU.not_equal, fill=1.0, base=0,
                                    pattern=[[-1, P]], channel_multiplier=1).then_inc(consts, 1)

            def general(l):
                S = L[l]

                def load(s, half):
                    for k in range(SB):
                        pool.dma_start(nat[:, half, k, :], adj_v[s * SB + k]).then_inc(
                            S[f"landed{half * SB + k}"], 16)

                load(0, 0)
                if l == 0:
                    extremes(0)
                load(1, 1)
                with pool.Fori(1, NS // 2) as J:
                    pool.wait_ge(S["turned"], J * 2 * NB - NB)
                    load(J * 2, 0)
                    pool.wait_ge(S["turned"], J * 2 * NB)
                    load(J * 2 + 1, 1)

            def extremes(l):
                S = L[l]
                pool.wait_ge(S["ext_ready"], 1)
                nc.gpsimd.partition_all_reduce(exta[:, 0:2], ext[:, 0:2], P, RMAX).then_inc(S["ext_all"], 1)

            def others():
                for l in range(1, LAYERS):
                    extremes(l)
                    general(l)
                    pool.drain().then_inc(L[l]["left"], 1)
                    if l + 1 < LAYERS:
                        pool.wait_ge(L[l]["go"], 1)
                        pool.drain()

            pool.wait_ge(loaded, 16 * 6)
            pool.wait_ge(entities_loaded, 16)
            pool.wait_ge(x_loaded, 16)
            general(0)
            pool.drain().then_inc(L[0]["left"], 1)
            pool.wait_ge(C["flags"], 1)
            nc.gpsimd.partition_all_reduce(exta[:, 3:4], ext[:, 2:3], P, RMAX).then_inc(C["flags_all"], 1)
            branch(pool, lambda: None, others)

        @block.tensor
        def _(pe):
            pe.wait_ge(setup_dve, 1)
            for m in range(2):
                nc.tensor.matmul(rowp[0][0:F, F * m:F * m + F], wmat[:, m, :], identf[0:F, 0:F],
                                 start=True, stop=True).then_inc(setup_pe, 1)
            pe.wait_ge(setup_dve, 2)
            for l in range(LAYERS):
                for t in range(2):
                    n = 2 * l + t
                    rhs = wt[:, l, :] if l < 2 else identf[0:F, 0:F]
                    mm = nc.tensor.matmul(rowp[1][:, F * n:F * n + F], arep[:, n, :], rhs, start=True, stop=True)
            mm.then_inc(setup_pe, 1)
            pe.wait_ge(setup_dve, 3)
            for m in range(2):
                nc.tensor.matmul(rowp[0][:, F * m:F * m + F], MT[:, :], wmat[:, 1, :] if m else identf[0:F, 0:F],
                                 start=True, stop=True).then_inc(setup_pe, 1)

            def colsums(l):
                S = L[l]
                V = h[src(l)]
                e = E[:, 1 if l == 1 else 0, :]
                for b in range(NB):
                    mm = nc.tensor.matmul(accp[0][0:F1, 0:P], V[:, b, :], onesf[:, :], start=(b == 0), stop=(b == NB - 1))
                mm.then_inc(S["cs_mm"], 1)
                pe.wait_ge(S["cs_ok"], 1)
                nc.tensor.matmul(accp[0][:, 0:F1], colsum[:, :], e, start=True, stop=True).then_inc(S["mr_mm"], 1)

            def row_product(m):
                pe.wait_ge(C["diags"], m + 1)
                if m >= 2:
                    pe.wait_ge(C["row_ok"], m - 1)
                nc.tensor.matmul(rowp[m % 2][:, :], onesf[:, :], diag[:, m % SB], start=True,
                                 stop=True).then_inc(C["row_mm"], 1)

            def tile(g, b):
                n = g * NB + b
                values = VW[(1 + g // 2) % 2]
                if b % HB == 0:
                    pe.wait_ge(C["vw_ready"], (g // 2) * 2 + 1 + b // HB)
                pe.wait_ge(C["tiles"], MR + n + 1)
                for c in range(SB):
                    a = F * (c % 2)
                    mm = nc.tensor.matmul(Wp[2 * (g % 2) + c // 2][a:a + F, :], values[:, b, :],
                                          T[:, n % TR, CW * c:CW * c + CW], start=(b == 0), stop=(b == NB - 1))
                mm.then_inc(C["used"], 1)

            def natural(g):
                e = 1 if 1 + g // 2 == 1 else 0
                pe.wait_ge(C["num_ok"], 2 * g + 2)
                for c in range(SB):
                    m = SB * g + c
                    if m >= 2:
                        pe.wait_ge(C["turned_ok"], m - 1)
                    a = F * (c % 2)
                    for k in range(SB):
                        at = CW * (c // 2) + P * k
                        mm = nc.tensor.matmul(accp[c % 2][:, F1 * k:F1 * k + F1],
                                              numF[a:a + F, at:at + P], EF[a:a + F, e, :], start=True, stop=True)
                    mm.then_inc(C["turned_mm"], 1)

            def fast():
                pe.sem_inc(C["used"], TR)
                for g in range(STEPS):
                    for b in range(NB):
                        tile(g, b)
                        if g and b == NATURAL_AT:
                            natural(g - 1)
                        if g + 2 < STEPS + 1 and b in ROWS_AT:
                            row_product(SB * (g + 1) + ROWS_AT.index(b))
                natural(STEPS - 1)

            def others():
                for l in range(1, LAYERS):
                    pe.wait_ge(hready, l + 1)
                    general(l)
                    pe.drain().then_inc(L[l]["left"], 1)
                    if l + 1 < LAYERS:
                        pe.wait_ge(L[l]["go"], 1)
                        pe.drain()

            def general(l):
                S = L[l]
                V = h[src(l)]
                e = E[:, 1 if l == 1 else 0, :]
                for c in range(N // CW):
                    pe.wait_ge(S["diag_d"], c + 1)
                    if c >= 2:
                        pe.wait_ge(S["drow_ok"], c - 1)
                    nc.tensor.matmul(rowp[c % 2][:, :], onesf[:, :], diag[:, c % SB], start=True, stop=True).then_inc(
                        S["drow_mm"], 1)
                colsums(l)

                def row_products(s):
                    pe.wait_ge(S["diag_ok"], s + 1)
                    for q in range(2):
                        nc.tensor.matmul(rowp[q][:, :], onesf[:, :], diag[:, q], start=True, stop=True).then_inc(
                            S["rows_mm"], 1)

                def turn(s, half, t, first=False):
                    if t == 0:
                        pe.wait_ge(S["binned"], s * SB + SB)
                    if not (first and t < RING):
                        pe.wait_ge(S["u_full"], s * NB + t - RING + 1)
                    for k in range(SB):
                        mm = nc.tensor.matmul(Wp[t % RING][:, P * k:P * k + P], nat_j[:, half, k, t, :],
                                              negb[:, :], start=(k == 0), stop=True, skip_group_check=True)
                    mm.then_inc(S["turned"], 1)

                def add_rows(s, half, t):
                    if t == 0:
                        pe.wait_ge(S["rows_ok"], s + 1)
                    pe.wait_ge(S["saved"], (s * NB + t + 1) * (CW // NB))
                    nc.tensor.matmul(Wp[t % RING][:, :], picks[:, :], s2rows[:, half, :], start=False,
                                     stop=True, skip_group_check=True).then_inc(S["w_full"], 1)

                def sum_values(s, half, b):
                    pe.wait_ge(S["p_full"], s * NB + b + 1)
                    mm = nc.tensor.matmul(accp[half][0:F1, :], V[:, b, :], U[:, b % URING, :], start=(b == 0),
                                          stop=(b == NB - 1))
                    if b == NB - 1:
                        mm.then_inc(S["acc_full"], 1)

                def natural(s, bank):
                    pe.wait_ge(S["numt_ok"], s + 1)
                    for k in range(SB):
                        mm = nc.tensor.matmul(bank[:, F1 * k:F1 * k + F1], numT[:, P * k:P * k + P], e,
                                              start=True, stop=True)
                    mm.then_inc(S["nat_mm"], 1)

                def super_block(s, half, first=False, last=False):
                    for t in range(LAG, NB):
                        turn(s, half, t)
                        add_rows(s, half, t - 1)
                        lags = LAST_LAGS if last else LAGS
                        for b in range(t - lags[t - 1], t + 1 - lags[t]):
                            sum_values(s, half, b)
                        if t == TURN_AT and not first:
                            natural(s - 1, rowp[0])
                        if t == PRODUCTS_AT and not last:
                            if not first:
                                pe.wait_ge(S["agg_ok"], s)
                            row_products(s + 1)
                    if last:
                        add_rows(s, half, NB - 1)
                        for b in range(NB - LAST_LAGS[-1], NB):
                            sum_values(s, half, b)
                        return
                    for t in range(LAG):
                        turn(s + 1, 1 - half, t)
                        if t == 0:
                            add_rows(s, half, NB - 1)
                        else:
                            add_rows(s + 1, 1 - half, t - 1)
                        for b in range(NB + t - LAGS[t - 1], NB + t + 1 - LAGS[t]):
                            sum_values(s, half, b)

                row_products(0)
                for t in range(LAG):
                    turn(0, 0, t, first=True)
                    if t:
                        add_rows(0, 0, t - 1)
                super_block(0, 0, first=True)
                with pe.Fori(0, NS // 2 - 1) as J:
                    super_block(J * 2 + 1, 1)
                    super_block(J * 2 + 2, 0)
                super_block(NS - 1, 1, last=True)
                if l == 0:
                    pe.wait_ge(S["agg_ok"], NS - 1)
                    for m in range(2):
                        row_product(m)
                natural(NS - 1, accp[0])

            pe.wait_ge(hready, 1)
            general(0)
            for m in range(2, SB):
                row_product(m)
            pe.drain().then_inc(L[0]["left"], 1)
            branch(pe, fast, others)

        @block.scalar
        def _(act):
            def colsums(l):
                S = L[l]
                act.wait_ge(S["cs_mm"], 1)
                nc.scalar.activation(colsum[:, :], accp[0][0:F1, 0:P], ACT.Copy).then_inc(S["cs_ok"], 1)
                act.wait_ge(S["mr_mm"], 1)
                nc.scalar.activation(meanrow[:, :], accp[0][:, 0:F1], ACT.Copy).then_inc(S["mr_ok"], 1)

            def blocks(half, one):
                for b in range(HB * half, HB * half + HB):
                    one(slice(b, b + 1))

            def negative_exp(f):
                l, half = parts(f)
                B = slice(HB * half, HB * half + HB)
                act.wait_ge(C["recips"], f + 1)
                nc.scalar.activation(tmp[:, B, 0:F], tmp[:, B, 0:F], ACT.Exp)
                act.drain().then_inc(C["activated"], 1)

            def close(f):
                l, half = parts(f)
                B = slice(HB * half, HB * half + HB)
                A, Z = agg, tmp
                if l:
                    g = f - 2
                    act.wait_ge(C["used"], TR + NB * (g + 1))
                    for b in range(2):
                        nc.scalar.activation(numF[:, CW * b:CW * b + CW], Wp[2 * half + b][:, :],
                                             ACT.Copy).then_inc(C["num_ok"], 1)
                    for c in range(SB):
                        act.wait_ge(C["turned_mm"], SB * g + c + 1)
                        s0 = SB * (SB * half + c)
                        nc.scalar.activation(agg[:, s0:s0 + SB, :], accp[c % 2][:, 0:SB * F1].rearrange(
                            "p (k f) -> p k f", k=SB), ACT.Copy).then_inc(C["turned_ok"], 1)
                if f == STEPS + 1:
                    return
                if l == 0:
                    negative_exp(f)
                else:
                    act.wait_ge(C["recips"], f + 1)
                    if OUTPUT[l] == ELU:
                        blocks(half, lambda b: nc.scalar.activation(Z[:, b, 0:F], A[:, b, 0:F], ACT.Relu,
                                                                    scale=fst[:, 1, b]))
                        act.drain()
                        nc.scalar.activation(Z[:, B, 0:F], Z[:, B, 0:F], ACT.Exp, scale=-1.0)
                    func = ACT.Copy if OUTPUT[l] == NONE else ACT.Relu
                    blocks(half, lambda b: nc.scalar.activation(A[:, b, 0:F], A[:, b, 0:F], func,
                                                                scale=fst[:, 0, b]))
                    act.drain().then_inc(C["activated"], 1)
                act.wait_ge(C["summed"], f + 1)
                blocks(half, lambda b: nc.scalar.activation(Z[:, b, 0:F], A[:, b, 0:F], ACT.Square,
                                                            bias=fst[:, 3, b], accum_out=fst[:, 4, b]))
                act.drain()
                nc.scalar.activation(fst[:, 6, B], fst[:, 4, B], ACT.Ln, scale=1.0 / F, bias=eps[:, 0:1])
                act.drain()
                nc.scalar.activation(fst[:, 7, B], fst[:, 6, B], ACT.Exp, scale=-0.5)
                act.drain().then_inc(C["squared"], 1)
                act.wait_ge(C["scaled"], f)
                blocks(half, lambda b: nc.scalar.activation(h[dst(l)][:, b, 0:F], A[:, b, 0:F], ACT.Identity,
                                                            scale=fst[:, 7, b], bias=fst[:, 8, b]))
                if l == LAYERS - 1:
                    act.drain().then_inc(C["half_out"], 1)
                    return
                act.drain().then_inc(C["normed"], 1)
                prepare(f)

            def column_weights(f):
                l, half = parts(f)
                B = slice(HB * half, HB * half + HB)
                slope = SLOPE[l + 1]
                act.wait_ge(C["d_ready"], f + 1)
                nc.scalar.activation(qcol[:, (l + 1) % 2, B], dless[:, B], ACT.Exp, scale=1.0 - slope).then_inc(
                    C["q_ready"], 1)
                nc.scalar.activation(wcol[:, B], dless[:, B], ACT.Exp, scale=slope)
                act.drain().then_inc(C["w_ready"], 1)

            def row_weights(f):
                l, half = parts(f)
                Z = tmp
                B = slice(HB * half, HB * half + HB)
                act.wait_ge(C["s_ready"], f + 1)
                if f:
                    blocks(half, lambda b: nc.scalar.activation(Z[:, b, 0:F], Z[:, b, 0:F], ACT.Copy,
                                                                accum_out=scol[:, b]))
                    act.drain()
                    nc.scalar.activation(scol[:, B], scol[:, B], ACT.Relu, bias=bound[:, 0, l:l + 1])
                    act.drain()
                nc.scalar.activation(rcol[:, B], scol[:, B], ACT.Exp, scale=SLOPE[l + 1] - 1.0)
                act.drain().then_inc(C["r_ready"], 1)

            def weights(f):
                column_weights(f)
                row_weights(f)

            def row(f, c):
                half, m = f % 2, SB * f + c
                act.wait_ge(C["row_mm"], m + 1)
                at = CW * (SB * half + c)
                nc.scalar.activation(drow[:, at:at + CW], rowp[m % 2][:, :], ACT.Copy).then_inc(C["row_ok"], 1)

            def prepare(f):
                l, half = parts(f)
                B = slice(HB * half, HB * half + HB)
                column_weights(f)
                blocks(half, lambda b: nc.scalar.activation(VW[(l + 1) % 2][:, b, 0:F - 1], h[dst(l)][:, b, 0:F - 1],
                                                            ACT.Copy, scale=wcol[:, b]))
                nc.scalar.activation(VW[(l + 1) % 2][:, B, F - 1:F], wcol[:, B].unsqueeze(2), ACT.Copy)
                act.drain().then_inc(C["vw_ready"], 1)
                row_weights(f)
                for c in range(SB):
                    for k in range(SB):
                        b = HB * half + SB * c + k
                        mm = nc.scalar.activation(diag[:, c, k, :], identf[:, :], ACT.Copy, scale=rcol[:, b:b + 1])
                    mm.then_inc(C["diags"], 1)
                for c in range(SB):
                    row(f, c)

            def fast():
                for f in range(1, STEPS + 2):
                    close(f)

            def others():
                exp_of_negative(0)
                for l in range(1, LAYERS):
                    general(l)
                    act.drain().then_inc(L[l]["left"], 1)
                    exp_of_negative(l)
                    if l + 1 < LAYERS:
                        act.wait_ge(L[l]["go"], 1)
                        act.drain()

            def exp_of_negative(l):
                S = L[l]
                if OUTPUT[l] == ELU:
                    act.wait_ge(S["elu_in"], 1)
                    b = slice(0 if l else HB, NB)
                    nc.scalar.activation(tmp[:, b, 0:F], tmp[:, b, 0:F], ACT.Exp).then_inc(S["elu_out"], 1)

            def general(l):
                S = L[l]
                for c in range(N // CW):
                    act.wait_ge(S["drow_mm"], c + 1)
                    nc.scalar.activation(drow_b[:, SB * c:SB * c + SB, :],
                                         rowp[c % 2][:, :].rearrange("p (b j) -> p b j", b=SB), ACT.Copy).then_inc(
                        S["drow_ok"], 1)
                colsums(l)

                def save(s, half, use, t):
                    if t == 0:
                        act.wait_ge(S[f"stored{half}"], use * 16 + 16)
                    act.wait_ge(S["turned"], s * NB + t + 1)
                    nc.scalar.activation(stg[:, half, t, :], Wp[t % RING][:, :], ACT.Relu,
                                         bias=1.0).then_inc(S["saved"], CW // NB)

                def exponential(s, b):
                    act.wait_ge(S["u_full"], s * NB + b + 1)
                    nc.scalar.activation(U[:, b % URING, :], U[:, b % URING, :], ACT.Exp,
                                         bias=dcol[:, b:b + 1]).then_inc(S["p_full"], 1)

                def evacuate_rows(s, half):
                    act.wait_ge(S["rows_mm"], 2 * s + 1)
                    nc.scalar.activation(s2hi[:, half, :], rowp[0][0:65, :], ACT.Copy).then_inc(S["rows_ev"], 1)
                    nc.scalar.activation(s2rows[0:1, half, :], rowp[0][0:1, :], ACT.Copy).then_inc(S["rows_ev"], 1)
                    act.wait_ge(S["rows_mm"], 2 * s + 2)
                    nc.scalar.activation(xrow[:, half, :], rowp[1][:, :], ACT.Copy).then_inc(S["rows_ev"], 1)

                def sums(s, half):
                    act.wait_ge(S["acc_full"], s + 1)
                    nc.scalar.activation(numT[:, :], accp[half][0:F1, :], ACT.Copy).then_inc(S["numt_ok"], 1)

                def turned_sums(s, bank):
                    act.wait_ge(S["nat_mm"], s + 1)
                    nc.scalar.activation(agg[:, bass.ts(s, SB), :],
                                         bank[:, 0:SB * F1].rearrange("p (k f) -> p k f", k=SB),
                                         ACT.Copy).then_inc(S["agg_ok"], 1)

                def super_block(s, half, use, first=False, last=False):
                    for t in range(2, NB):
                        save(s, half, use, t)
                        exponential(s, t - 2)
                        if t == SUMS_AT and not first:
                            sums(s - 1, 1 - half)
                        if t == TURNED_AT and not first:
                            turned_sums(s - 1, rowp[0])
                        if t == EVACUATE_AT and not last:
                            evacuate_rows(s + 1, 1 - half)
                        if t == ALONE_EXP_AT and last and l == 0:
                            negative_exp(0)
                    for t in range(2):
                        if not last:
                            save(s + 1, 1 - half, use + (1 if half else 0), t)
                        exponential(s, NB - 2 + t)

                evacuate_rows(0, 0)
                for t in range(2):
                    save(0, 0, 0, t)
                super_block(0, 0, 0, first=True)
                with act.Fori(0, NS // 2 - 1) as J:
                    super_block(J * 2 + 1, 1, J)
                    super_block(J * 2 + 2, 0, J + 1)
                super_block(NS - 1, 1, NS // 2 - 1, last=True)
                if l == 0:
                    weights(0)
                sums(NS - 1, 1)
                if l == 0:
                    for c in range(2):
                        row(0, c)
                turned_sums(NS - 1, accp[0])

            general(0)
            for c in range(2, SB):
                row(0, c)
            act.drain().then_inc(L[0]["left"], 1)
            branch(act, fast, others)

        @block.vector
        def _(dve):
            v = nc.vector

            def newton(y, x, t):
                v.scalar_tensor_tensor(out=t, in0=t, scalar=-0.5, in1=x, op0=ALU.mult, op1=ALU.mult)
                dve.drain()
                v.scalar_tensor_tensor(out=y, in0=t, scalar=1.5, in1=y, op0=ALU.add, op1=ALU.mult)
                dve.drain()

            def rsqrt(y, x, t):
                v.tensor_scalar(t.bitcast(I32), x.bitcast(I32), 1, None, ALU.logical_shift_right)
                dve.drain()
                v.tensor_scalar(y.bitcast(I32), t.bitcast(I32), -1.0, MAGIC, ALU.mult, ALU.add)
                dve.drain()
                for _ in range(3):
                    v.tensor_tensor(t, y, y, ALU.mult)
                    dve.drain()
                    newton(y, x, t)

            def rows_of(col, n):
                return col.unsqueeze(2).to_broadcast([P, n, F])

            def dots(l, t):
                node, col = ((h[res(l)], scol), (h[src(l)], dcol))[t]
                v.tensor_tensor(tmp[:, :, 0:F], node[:, :, 0:F],
                                wrow[:, l, t, :].unsqueeze(1).to_broadcast([P, NB, F]), ALU.mult)
                dve.drain()
                v.tensor_reduce(col[:, :], tmp[:, :, 0:F], AX.X, ALU.add)
                dve.drain()

            def column_scores(l):
                dots(l, 1)
                v.tensor_reduce(ext[:, 0:1], dcol[:, :], AX.X, ALU.max)
                v.tensor_reduce(ext[:, 1:2], dcol[:, :], AX.X, ALU.min, negate=True)
                dve.drain().then_inc(L[l]["ext_ready"], 1)
                v.tensor_scalar(ycol[:, :], dcol[:, :], -(1.0 - SLOPE[l]), None, ALU.mult)

            def row_scores_of(l):
                dots(l, 0)
                dve.drain().then_inc(hready, 1)

            v.memset(onesf[:], 1.0)
            v.memset(eps[:], EPS)
            v.memset(picks[:], 0.0)
            v.memset(s2rows[:], 0.0)
            for b in range(2):
                v.memset(h[b][:, :, F:F1], 1.0)
            dve.drain()
            for r in (0, 32, 64):
                v.memset(picks[r:r + 1, :], 1.0)
            dve.wait_ge(consts, 2)
            v.tensor_scalar(negb[:], identf[:], -1.0, None, ALU.mult)
            dve.wait_ge(loaded, 16 * 6)
            for m in range(2):
                v.tensor_copy(E[:, m, :], identf[0:F1, 0:F1])
            dve.drain()
            v.tensor_copy(E[0:F, 1, 0:F], wmat[:, 1, :])
            dve.drain().then_inc(setup_dve, 1)
            dve.wait_ge(setup_pe, 2)
            v.tensor_copy(wt[:, :, :], rowp[0][0:F, 0:2 * F].rearrange("p (m f) -> p m f", m=2))
            v.tensor_tensor(arep[:, :, :], onesf[0:F, :].unsqueeze(1).to_broadcast([F, 2 * LAYERS, P]),
                            acol[:, :, :].rearrange("f l t -> f (l t)").unsqueeze(2).to_broadcast(
                                [F, 2 * LAYERS, P]), ALU.mult)
            dve.drain().then_inc(setup_dve, 1)
            last = identf[0:F, F - 1:F]
            for q in range(2):
                v.tensor_scalar(MT[:, F * q:F * q + F - 1], identf[0:F, 0:F - 1], last, None, ALU.subtract)
                v.memset(MT[:, F * q + F - 1:F * q + F], 0.0)
            dve.drain().then_inc(setup_dve, 1)
            dve.wait_ge(setup_pe, 3)
            v.tensor_copy(wrow[:, :, :, :].rearrange("p l t f -> p (l t f)"), rowp[1][:, :])
            dve.drain()
            dve.wait_ge(entities_loaded, 16)
            column_scores(0)
            dve.wait_ge(setup_pe, 5)
            v.tensor_copy(EF[:, :, 0:F], rowp[0][:, 0:2 * F].rearrange("p (m f) -> p m f", m=2))
            for m in range(2):
                v.tensor_tensor(EF[:, m, F:F1], identf[:, F - 1:F], identf[:, P - 1:P], ALU.add)
            v.tensor_tensor(tmp[:, 0:LAYERS - 1, 0:F], wrow[:, 1:LAYERS, 1, :], wrow[:, 1:LAYERS, 1, :], ALU.mult)
            dve.drain()
            v.tensor_reduce(bound[:, 1, :], tmp[:, 0:LAYERS - 1, 0:F], AX.X, ALU.add)
            dve.drain()
            v.tensor_scalar(bound[:, 2, :], bound[:, 1, :], 1e-30, None, ALU.add)
            dve.drain()
            rsqrt(bound[:, 3, :], bound[:, 2, :], bound[:, 4, :])
            v.scalar_tensor_tensor(out=bound[:, 0, :], in0=bound[:, 1, :], scalar=1.01 * F ** 0.5,
                                   in1=bound[:, 3, :], op0=ALU.mult, op1=ALU.mult)
            dve.drain()
            v.tensor_reduce(bound[:, 5, 0:1], bound[:, 0, :], AX.X, ALU.max)
            dve.wait_ge(x_loaded, 16)
            row_scores_of(0)

            def bounds(l):
                S = L[l]
                dve.wait_ge(S["ext_all"], 1)
                v.tensor_tensor(ext[:, 2:3], exta[:, 0:1], exta[:, 1:2], ALU.add)
                dve.drain()
            def invert(f):
                l, half = parts(f)
                B = slice(HB * half, HB * half + HB)
                if l:
                    dve.wait_ge(C["turned_ok"], SB * (f - 1))
                v.reciprocal(fst[:, 0, B], agg[:, B, F:F1].rearrange("p b o -> p (b o)"))
                dve.drain()
                if f == STEPS + 1:
                    v.tensor_tensor(agg[:, B, 0:F], agg[:, B, 0:F], rows_of(fst[:, 0, B], HB), ALU.mult)
                    dve.drain()
                    return
                if OUTPUT[l] == ELU and l:
                    v.tensor_scalar(fst[:, 1, B], fst[:, 0, B], -1.0, None, ALU.mult)
                if l == 0:
                    A = agg[:, B, 0:F]
                    v.tensor_tensor(A, A, rows_of(fst[:, 0, B], HB), ALU.mult)
                    dve.drain()
                    v.tensor_tensor(A, A, h[res(0)][:, B, 0:F], ALU.add)
                    dve.drain()
                    v.tensor_scalar(tmp[:, B, 0:F], A, 0.0, None, ALU.min)
                dve.drain().then_inc(C["recips"], 1)

            def add_up(f):
                l, half = parts(f)
                B = slice(HB * half, HB * half + HB)
                A, Z, H = agg[:, B, 0:F], tmp[:, B, 0:F], h[res(l)][:, B, 0:F]
                if f <= STEPS:
                    dve.wait_ge(C["activated"], f + 1)
                if f == STEPS + 1:
                    v.scalar_tensor_tensor(out=A, in0=A, scalar=0.0, in1=H, op0=ALU.max, op1=ALU.add)
                elif OUTPUT[l] == ELU:
                    v.scalar_tensor_tensor(out=A, in0=A, scalar=0.0, in1=Z, op0=ALU.max, op1=ALU.add)
                    dve.drain()
                    v.scalar_tensor_tensor(out=A, in0=A, scalar=-1.0, in1=H, op0=ALU.add, op1=ALU.add)
                else:
                    v.tensor_tensor(A, A, H, ALU.add)
                dve.drain()
                v.tensor_reduce(fst[:, 2, B], A, AX.X, ALU.add)
                dve.drain()
                v.tensor_scalar(fst[:, 3, B], fst[:, 2, B], -1.0 / F, None, ALU.mult)
                dve.drain().then_inc(C["summed"], 1)

            def deviations(f):
                l, half = parts(f)
                B = slice(HB * half, HB * half + HB)
                dve.wait_ge(C["squared"], f)
                v.tensor_scalar(fst[:, 5, B], fst[:, 4, B], 1.0 / F, EPS, ALU.mult, ALU.add)
                v.tensor_tensor(fst[:, 6, B], fst[:, 7, B], fst[:, 7, B], ALU.mult)
                dve.drain()
                newton(fst[:, 7, B], fst[:, 5, B], fst[:, 6, B])
                v.tensor_tensor(fst[:, 8, B], fst[:, 7, B], fst[:, 3, B], ALU.mult)
                dve.drain().then_inc(C["scaled"], 1)

            def half_score(f, t, col):
                l, half = parts(f)
                B = slice(HB * half, HB * half + HB)
                v.tensor_tensor(tmp[:, B, 0:F], h[dst(l)][:, B, 0:F],
                                wrow[:, l + 1, t, :].unsqueeze(1).to_broadcast([P, HB, F]), ALU.mult)
                dve.drain()
                v.tensor_reduce(col[:, B], tmp[:, B, 0:F], AX.X, ALU.add)
                dve.drain()

            def columns(f):
                l, half = parts(f)
                B = slice(HB * half, HB * half + HB)
                if f:
                    dve.wait_ge(C["normed"], f)
                half_score(f, 1, dless)
                v.tensor_scalar(dless[:, B], dless[:, B], bound[:, 0, l:l + 1], None, ALU.subtract)
                dve.drain().then_inc(C["d_ready"], 1)

            def row_scores(f):
                l, half = parts(f)
                B = slice(HB * half, HB * half + HB)
                if f == 0:
                    half_score(f, 0, scol)
                    v.tensor_scalar(scol[:, B], scol[:, B], bound[:, 0, l:l + 1], 0.0, ALU.add, ALU.max)
                else:
                    v.tensor_tensor(tmp[:, B, 0:F], h[dst(l)][:, B, 0:F],
                                    wrow[:, l + 1, 0, :].unsqueeze(1).to_broadcast([P, HB, F]), ALU.mult)
                dve.drain().then_inc(C["s_ready"], 1)

            def patch(f):
                l, half = parts(f)
                B = slice(HB * half, HB * half + HB)
                dve.wait_ge(L[l]["mr_ok"], 1)
                dve.wait_ge(L[l]["agg_ok"], SB * (half + 1))
                v.tensor_scalar(st[:, 0, B], agg[:, B, F:F1].rearrange("p b o -> p (b o)"), 0.0, None, ALU.is_le)
                dve.drain()
                v.tensor_tensor(tmp[:, B, :], st[:, 0, B].unsqueeze(2).to_broadcast([P, HB, F1]),
                                meanrow[:, :].unsqueeze(1).to_broadcast([P, HB, F1]), ALU.mult)
                dve.drain()
                v.tensor_tensor(agg[:, B, :], agg[:, B, :], tmp[:, B, :], ALU.add)
                dve.drain()

            def center(f):
                l, half = parts(f)
                B = slice(HB * half, HB * half + HB)
                A, Z = agg[:, B, 0:F], tmp[:, B, 0:F]
                v.tensor_tensor(A, A, rows_of(fst[:, 3, B], HB), ALU.add)
                dve.drain()
                v.tensor_tensor(Z, A, A, ALU.mult)
                dve.drain()
                v.tensor_reduce(fst[:, 4, B], Z, AX.X, ALU.add)
                dve.drain()
                v.tensor_scalar(fst[:, 5, B], fst[:, 4, B], 1.0 / F, EPS, ALU.mult, ALU.add)
                dve.drain()

            def norm(f):
                l, half = parts(f)
                B = slice(HB * half, HB * half + HB)
                A, Z = agg[:, B, 0:F], tmp[:, B, 0:F]
                rsqrt(fst[:, 7, B], fst[:, 5, B], fst[:, 6, B])
                v.tensor_tensor(h[dst(l)][:, B, 0:F], A, rows_of(fst[:, 7, B], HB), ALU.mult)
                dve.drain()

            STAGES = (invert, add_up, deviations, columns, row_scores)

            def tile(g, n, slot):
                half, par = g % 2, (1 + g // 2) % 2
                dve.wait_ge(C[f"mask{slot}"], (n // MR) * 16 + 16 * (g * NB // MR + 1))
                dve.wait_ge(C["used"], n + slot + g * NB + 1)
                col = qcol[:, par, bass.ds(n + slot, 1)]
                v.scalar_tensor_tensor(
                    out=T[:, slot, :], in0=drow[:, HALF * half:HALF * half + HALF],
                    scalar=col, in1=mring[:, slot, :],
                    op0=ALU.max, op1=ALU.mult).then_inc(C["tiles"], 1)

            def step(g):
                f = g + 1
                dve.wait_ge(C["row_ok"], SB * (g + 1))
                for n in range(LOOP_AT):
                    if n == 0:
                        dve.wait_ge(C["q_ready"], g // 2 * 2 + 1)
                    if n == HB:
                        dve.wait_ge(C["q_ready"], g // 2 * 2 + 2)
                    tile(g, n - n % MR, n % MR)
                    for at, stage in zip(DVE_AT[f // 2], STAGES):
                        if at == n + 1:
                            if f < 2 * LAYERS - 2 or stage in STAGES[:3]:
                                stage(f)
                with dve.Fori(LOOP_AT, NB - MR + 1, MR) as n:
                    for u in range(MR):
                        tile(g, n, u)

            def fast():
                dve.sem_inc(C["tiles"], MR)
                for g in range(STEPS):
                    step(g)
                for stage in (invert, add_up, center, norm):
                    stage(STEPS + 1)
                dve.drain().then_inc(C["half_out"], 1)

            def general(l):
                S = L[l]
                slope = SLOPE[l]
                for c in range(NB // SB):
                    if c >= SB:
                        dve.wait_ge(S["drow_mm"], c - SB + 1)
                    v.tensor_tensor(diag[:, c % SB], identf[:, :].unsqueeze(1).to_broadcast([P, SB, P]),
                                    dcol[:, SB * c:SB * c + SB].unsqueeze(2).to_broadcast([P, SB, P]),
                                    ALU.mult).then_inc(S["diag_d"], 1)
                bounds(l)
                v.tensor_scalar(ext[:, 3:4], ext[:, 2:3], 2.0, 256.0, ALU.mult, ALU.add)
                v.tensor_scalar(exta[:, 2:3], exta[:, 1:2], -1.0, None, ALU.mult)
                dve.drain()
                dve.wait_ge(S["drow_ok"], N // CW)
                dve.wait_ge(S["drow_mm"], N // CW)

                def binarise(half, k, turn):
                    dve.wait_ge(S[f"landed{half * SB + k}"], turn)
                    v.tensor_scalar(nat[:, half, k, :], nat[:, half, k, :], 0.0, ext[:, 3:4], ALU.is_le, ALU.mult)
                    dve.drain().then_inc(S["binned"], 1)

                def row_max(half, k, c):
                    dve.drain()
                    v.tensor_tensor_reduce(junk[:, :], drow[:, CHUNK * c:CHUNK * c + CHUNK],
                                           nat[:, half, k, CHUNK * c:CHUNK * c + CHUNK], 1.0, -3.0e38,
                                           ALU.subtract, ALU.max,
                                           rmax[:, k, c:c + 1])

                def row_terms(s):
                    dve.drain()
                    v.tensor_reduce(sm[:, 0, :], rmax[:, :, :], AX.X, ALU.max)
                    dve.drain()
                    v.tensor_scalar(sm[:, 1, :], sm[:, 0, :], exta[:, 2:3], None, ALU.max)
                    dve.drain()
                    sc = scol[:, bass.ts(s, SB)]
                    v.tensor_tensor(sm[:, 2, :], sm[:, 1, :], sc, ALU.add)
                    dve.drain()
                    v.scalar_tensor_tensor(out=sm[:, 3, :], in0=sm[:, 2, :], scalar=slope, in1=sm[:, 2, :],
                                           op0=ALU.mult, op1=ALU.max)
                    dve.drain()
                    v.scalar_tensor_tensor(out=sm[:, 4, :], in0=sc, scalar=slope, in1=sm[:, 3, :],
                                           op0=ALU.mult, op1=ALU.subtract)
                    v.tensor_scalar(sm[:, 5, :], sc, 1.0 - slope, None, ALU.mult)
                    dve.drain()
                    v.tensor_tensor(diag[:, 0:2].rearrange("p q k j -> p (q k) j"),
                                    identf[:, :].unsqueeze(1).to_broadcast([P, 2 * SB, P]),
                                    sm[:, 4:6, :].rearrange("p q k -> p (q k)").unsqueeze(2).to_broadcast(
                                        [P, 2 * SB, P]), ALU.mult).then_inc(S["diag_ok"], 1)

                def split(s, half):
                    dve.wait_ge(S["rows_ev"], 3 * s + 2)
                    v.tensor_tensor(s2r[:, :], rowp[0][0:65, :], s2hi[:, half, :], ALU.subtract)
                    dve.drain()
                    v.tensor_copy(s2mid[:, :], s2r[:, :])
                    dve.drain()
                    v.tensor_copy(s2rows[32:33, half, :], s2mid[32:33, :])
                    dve.wait_ge(S["rows_ev"], 3 * s + 3)
                    v.tensor_tensor(s2rows[64:65, half, :], s2r[64:65, :], s2mid[64:65, :], ALU.subtract)
                    dve.drain().then_inc(S["rows_ok"], 1)

                def super_block(s, half, use, last=False):
                    for t in range(NB):
                        dve.wait_ge(S["w_full"], s * NB + t + 1)
                        v.scalar_tensor_tensor(out=U[:, t % URING, :], in0=xrow[:, half, :], scalar=ycol[:, t:t + 1],
                                               in1=Wp[t % RING][:, :], op0=ALU.max,
                                               op1=ALU.add).then_inc(S["u_full"], 1)
                        if last:
                            if l == 0 and t in HOOKS0:
                                (patch, invert, add_up, center, norm, columns, row_scores)[HOOKS0.index(t)](0)
                            continue
                        k, at = t // 6, t % 6
                        if k < SB and at == 0:
                            binarise(1 - half, k, use * 16 + 16)
                        if k < SB and at in (2, 4):
                            row_max(1 - half, k, at // 2 - 1)
                        if t == TERMS_AT:
                            row_terms(s + 1)
                        if t == SPLIT_AT:
                            split(s + 1, 1 - half)

                for k in range(SB):
                    binarise(0, k, 16)
                    for c in range(NCH):
                        row_max(0, k, c)
                row_terms(0)
                split(0, 0)
                super_block(0, 0, 0)
                with dve.Fori(0, NS // 2 - 1) as J:
                    super_block(J * 2 + 1, 1, J + 1)
                    super_block(J * 2 + 2, 0, J + 1)
                super_block(NS - 1, 1, 0, last=True)

            def output(l, B):
                S = L[l]
                n = len(range(*B.indices(NB)))
                den = agg[:, B, F:F1].rearrange("p b o -> p (b o)")
                v.tensor_scalar(st[:, 0, B], den, 0.0, None, ALU.is_le)
                dve.drain()
                v.tensor_tensor(tmp[:, B, :], st[:, 0, B].unsqueeze(2).to_broadcast([P, n, F1]),
                                meanrow[:, :].unsqueeze(1).to_broadcast([P, n, F1]), ALU.mult)
                dve.drain()
                v.tensor_tensor(agg[:, B, :], agg[:, B, :], tmp[:, B, :], ALU.add)
                dve.drain()
                v.reciprocal(st[:, 1, B], den)
                dve.drain()
                A = agg[:, B, 0:F]
                Z = tmp[:, B, 0:F]
                H = h[res(l)][:, B, 0:F]
                v.tensor_tensor(A, A, rows_of(st[:, 1, B], n), ALU.mult)
                dve.drain()
                if l == 0:
                    v.tensor_tensor(A, A, H, ALU.add)
                    dve.drain()
                if OUTPUT[l] == ELU:
                    v.tensor_scalar(Z, A, 0.0, None, ALU.min)
                    dve.drain().then_inc(S["elu_in"], 1)
                    dve.wait_ge(S["elu_out"], 1)
                    v.scalar_tensor_tensor(out=A, in0=A, scalar=0.0, in1=Z, op0=ALU.max, op1=ALU.add)
                    dve.drain()
                    v.scalar_tensor_tensor(out=A, in0=A, scalar=-1.0, in1=H, op0=ALU.add, op1=ALU.add)
                elif OUTPUT[l] == RELU:
                    v.scalar_tensor_tensor(out=A, in0=A, scalar=0.0, in1=H, op0=ALU.max, op1=ALU.add)
                else:
                    v.tensor_tensor(A, A, H, ALU.add)
                dve.drain()
                v.tensor_reduce(st[:, 2, B], A, AX.X, ALU.add)
                dve.drain()
                v.tensor_scalar(st[:, 3, B], st[:, 2, B], 1.0 / F, None, ALU.mult)
                dve.drain()
                v.tensor_tensor(A, A, rows_of(st[:, 3, B], n), ALU.subtract)
                dve.drain()
                v.tensor_tensor(Z, A, A, ALU.mult)
                dve.drain()
                v.tensor_reduce(st[:, 4, B], Z, AX.X, ALU.add)
                dve.drain()
                v.tensor_scalar(st[:, 5, B], st[:, 4, B], 1.0 / F, EPS, ALU.mult, ALU.add)
                dve.drain()
                rsqrt(st[:, 7, B], st[:, 5, B], st[:, 6, B])
                v.tensor_tensor(h[dst(l)][:, B, 0:F], A, rows_of(st[:, 7, B], n), ALU.mult)
                dve.drain()
                if l == LAYERS - 1:
                    dve.drain().then_inc(C["half_out"], 2)

            def leave(l):
                S = L[l]
                dve.wait_ge(S["agg_ok"], NS)
                dve.wait_ge(S["mr_ok"], 1)
                dve.drain().then_inc(S["left"], 1)

            def others():
                output(0, slice(HB, NB))
                for l in range(1, LAYERS):
                    column_scores(l)
                    row_scores_of(l)
                    general(l)
                    leave(l)
                    output(l, slice(0, NB))
                    if l + 1 < LAYERS:
                        dve.wait_ge(L[l]["go"], 1)
                        dve.drain()

            general(0)
            dve.wait_ge(C["r_ready"], 1)
            dve.wait_ge(C["w_ready"], 1)
            B0 = slice(0, HB)
            for c in range(SB):
                v.tensor_tensor(diag[:, c], identf[:, :].unsqueeze(1).to_broadcast([P, SB, P]),
                                rcol[:, SB * c:SB * c + SB].unsqueeze(2).to_broadcast([P, SB, P]),
                                ALU.mult).then_inc(C["diags"], 1)
            v.tensor_tensor(VW[1][:, B0, 0:F - 1], h[0][:, B0, 0:F - 1],
                            wcol[:, B0].unsqueeze(2).to_broadcast([P, HB, F - 1]), ALU.mult)
            v.tensor_copy(VW[1][:, B0, F - 1:F], wcol[:, B0].unsqueeze(2))
            dve.drain().then_inc(C["vw_ready"], 1)
            leave(0)
            v.tensor_scalar(st[:, 0, HB:NB], agg[:, HB:NB, F:F1].rearrange("p b o -> p (b o)"), 0.0, None,
                            ALU.is_le)
            dve.drain()
            v.tensor_reduce(ext[:, 2:3], st[:, 0, :], AX.X, ALU.max)
            dve.drain().then_inc(C["flags"], 1)
            dve.wait_ge(C["flags_all"], 1)
            v.tensor_scalar(ext[:, 3:4], exta[:, 3:4], 1.0e6, None, ALU.mult)
            dve.drain()
            v.tensor_tensor(ext[:, 2:3], ext[:, 3:4], bound[:, 5, 0:1], ALU.add)
            dve.drain()
            v.tensor_scalar(choice[:, :], ext[:, 2:3], MAX_BOUND, None, ALU.is_le)
            dve.drain().then_inc(C["choice"], 1)
            branch(dve, fast, others)


_INS = ["x", "adj", "L0_gnn_entity_embs", "L0_gnn_W", "L0_gnn_a", "L1_gnn_W", "L1_gnn_a", "L2_gnn_a", "L3_gnn_a"]


def kernel(**inputs):
    import numpy as _np
    import concourse.bacc as _bacc
    from concourse import mybir as _mybir
    from concourse.bass_utils import run_bass_kernel_spmd as _run

    nc = _bacc.Bacc("TRN2", target_bir_lowering=False, num_devices=1)
    arrays, args = {}, []
    for name in _INS:
        a = _np.ascontiguousarray(inputs[name])
        arrays[f"in_{name}_dram"] = a
        args.append(nc.dram_tensor(f"in_{name}_dram", a.shape, _mybir.dt.from_np(a.dtype), kind="ExternalInput").ap())
    shape = inputs["x"].shape
    res = nc.dram_tensor("out_dram", shape, _mybir.dt.float32, kind="ExternalOutput").ap()
    build(nc, *args, res)
    r = _run(nc, [arrays], core_ids=[0])
    return r.results[0]["out_dram"]
```
